# Optimizing a Trainium2 kernel written in Bass

```python
import numpy as np
import jax
import jax.numpy as jnp

def _softmax(x, axis=-1):
    return jax.nn.softmax(x, axis=axis)

def _gelu(x):
    return jax.nn.gelu(x, approximate=True)

def _silu(x):
    return jax.nn.silu(x)

def _sigmoid(x):
    return jax.nn.sigmoid(x)

def _layernorm(x, axis=-1, eps=1e-05):
    m = jnp.mean(x, axis=axis, keepdims=True)
    v = jnp.var(x, axis=axis, keepdims=True)
    return (x - m) / jnp.sqrt(v + eps)

def _scatter_add(tgt, idx, src, axis=0):
    return tgt.at[idx].add(src)

def _segment_sum(src, seg, n):
    return jax.ops.segment_sum(src, seg, n)
kernel_name = 'mk_gnn_preln_d1_gnn_r8_248974'

def setup_inputs(seed: int=0):
    np.random.seed(seed)
    _w = jnp.asarray

    def _rec_inputs():
        import jax
        import jax.numpy as jnp
        _gk = jax.random.key(seed)
        x = -0.0005121 + 1.001 * jax.random.normal(jax.random.fold_in(_gk, 1), (12500, 64), jnp.float32)
        src = jax.random.randint(jax.random.fold_in(_gk, 2), (200000,), 0, 12500, jnp.int32)
        dst = jax.random.randint(jax.random.fold_in(_gk, 3), (200000,), 0, 12500, jnp.int32)
        _o = jnp.argsort(dst, stable=True)
        src = src[_o]
        dst = dst[_o]
        edge_attr_64 = -9.77346e-05 + 0.999888 * jax.random.normal(jax.random.fold_in(_gk, 11), (200000, 64), jnp.float32)
        return (x, src, dst, edge_attr_64)
    x, src, dst, edge_attr_64 = _rec_inputs()

    def _L0_gnn_setup():
        import jax, jax.numpy as jnp
        import numpy as np
        N, E, D, H, L = (6250, 100000, 64, 4, 2)
        DH = D // H

        def layer_norm(h, g, b, eps=1e-05):
            mu = h.mean(-1, keepdims=True)
            var = ((h - mu) ** 2).mean(-1, keepdims=True)
            return (h - mu) / jnp.sqrt(var + eps) * g + b

        def exphormer_layer(h, edge_attr, src, dst, p):
            wq, wk, we, wv, wo, bo, g1, be1, w1, b1, w2, b2, g2, be2 = p
            n = h.shape[0]
            Qh = (h @ wq).reshape(n, H, DH)
            Kh = (h @ wk).reshape(n, H, DH)
            Vh = (h @ wv).reshape(n, H, DH)
            Eh = (edge_attr @ we).reshape(-1, H, DH)
            s = jnp.sum(Kh[src] * Qh[dst] * Eh, axis=-1, keepdims=True) / np.sqrt(DH)
            score = jnp.exp(jnp.clip(s, -5.0, 5.0))
            msg = Vh[src] * score
            wV = jax.ops.segment_sum(msg, dst, num_segments=n)
            Z = jax.ops.segment_sum(score, dst, num_segments=n)
            h_attn = (wV / (Z + 1e-06)).reshape(n, D)
            h1 = layer_norm(h + (h_attn @ wo + bo), g1, be1)
            ffn = jax.nn.relu(h1 @ w1 + b1) @ w2 + b2
            return layer_norm(h1 + ffn, g2, be2)
        key = jax.random.key(seed)
        ks = jax.random.split(key, 16)
        s = 1.0 / np.sqrt(D)
        inp = {'x': jax.random.normal(ks[0], (N, D), jnp.float32), 'edge_attr': jax.random.normal(ks[1], (E, D), jnp.float32), 'edge_index': jax.random.randint(ks[2], (2, E), 0, N, jnp.int64), 'WQ': jax.random.normal(ks[3], (L, D, D), jnp.float32) * s, 'WK': jax.random.normal(ks[4], (L, D, D), jnp.float32) * s, 'WE': jax.random.normal(ks[5], (L, D, D), jnp.float32) * s, 'WV': jax.random.normal(ks[6], (L, D, D), jnp.float32) * s, 'WO': jax.random.normal(ks[7], (L, D, D), jnp.float32) * s, 'bO': jnp.zeros((L, D), jnp.float32), 'ln1_g': jnp.ones((L, D), jnp.float32), 'ln1_b': jnp.zeros((L, D), jnp.float32), 'W1': jax.random.normal(ks[8], (L, D, 2 * D), jnp.float32) * s, 'b1': jnp.zeros((L, 2 * D), jnp.float32), 'W2': jax.random.normal(ks[9], (L, 2 * D, D), jnp.float32) * (1.0 / np.sqrt(2 * D)), 'b2': jnp.zeros((L, D), jnp.float32), 'ln2_g': jnp.ones((L, D), jnp.float32), 'ln2_b': jnp.zeros((L, D), jnp.float32)}
        return inp
    _L0_gnn_all = _L0_gnn_setup()
    _L0_gnn_in = {k: v for k, v in _L0_gnn_all.items() if k in ('WQ', 'WK', 'WE', 'WV', 'WO', 'bO', 'ln1_g', 'ln1_b', 'W1', 'b1', 'W2', 'b2', 'ln2_g', 'ln2_b')}
    del _L0_gnn_all
    return {'x': x, 'src': src, 'dst': dst, 'edge_attr_64': edge_attr_64, 'L0_gnn_WQ': _L0_gnn_in['WQ'], 'L0_gnn_WK': _L0_gnn_in['WK'], 'L0_gnn_WE': _L0_gnn_in['WE'], 'L0_gnn_WV': _L0_gnn_in['WV'], 'L0_gnn_WO': _L0_gnn_in['WO'], 'L0_gnn_bO': _L0_gnn_in['bO'], 'L0_gnn_ln1_g': _L0_gnn_in['ln1_g'], 'L0_gnn_ln1_b': _L0_gnn_in['ln1_b'], 'L0_gnn_W1': _L0_gnn_in['W1'], 'L0_gnn_b1': _L0_gnn_in['b1'], 'L0_gnn_W2': _L0_gnn_in['W2'], 'L0_gnn_b2': _L0_gnn_in['b2'], 'L0_gnn_ln2_g': _L0_gnn_in['ln2_g'], 'L0_gnn_ln2_b': _L0_gnn_in['ln2_b']}

def reference(x, src, dst, edge_attr_64, L0_gnn_WQ, L0_gnn_WK, L0_gnn_WE, L0_gnn_WV, L0_gnn_WO, L0_gnn_bO, L0_gnn_ln1_g, L0_gnn_ln1_b, L0_gnn_W1, L0_gnn_b1, L0_gnn_W2, L0_gnn_b2, L0_gnn_ln2_g, L0_gnn_ln2_b):
    import jax
    import jax.numpy as jnp

    def _L0_gnn_ref(x, edge_attr, edge_index, WQ, WK, WE, WV, WO, bO, ln1_g, ln1_b, W1, b1, W2, b2, ln2_g, ln2_b):
        import jax, jax.numpy as jnp
        import numpy as np
        N, E, D, H, L = (6250, 100000, 64, 4, 2)
        DH = D // H

        def layer_norm(h, g, b, eps=1e-05):
            mu = h.mean(-1, keepdims=True)
            var = ((h - mu) ** 2).mean(-1, keepdims=True)
            return (h - mu) / jnp.sqrt(var + eps) * g + b

        def exphormer_layer(h, edge_attr, src, dst, p):
            wq, wk, we, wv, wo, bo, g1, be1, w1, b1, w2, b2, g2, be2 = p
            n = h.shape[0]
            Qh = (h @ wq).reshape(n, H, DH)
            Kh = (h @ wk).reshape(n, H, DH)
            Vh = (h @ wv).reshape(n, H, DH)
            Eh = (edge_attr @ we).reshape(-1, H, DH)
            s = jnp.sum(Kh[src] * Qh[dst] * Eh, axis=-1, keepdims=True) / np.sqrt(DH)
            score = jnp.exp(jnp.clip(s, -5.0, 5.0))
            msg = Vh[src] * score
            wV = jax.ops.segment_sum(msg, dst, num_segments=n)
            Z = jax.ops.segment_sum(score, dst, num_segments=n)
            h_attn = (wV / (Z + 1e-06)).reshape(n, D)
            h1 = layer_norm(h + (h_attn @ wo + bo), g1, be1)
            ffn = jax.nn.relu(h1 @ w1 + b1) @ w2 + b2
            return layer_norm(h1 + ffn, g2, be2)
        src = edge_index[0]
        dst = edge_index[1]
        h = x
        for l in range(L):
            p = (WQ[l], WK[l], WE[l], WV[l], WO[l], bO[l], ln1_g[l], ln1_b[l], W1[l], b1[l], W2[l], b2[l], ln2_g[l], ln2_b[l])
            h = exphormer_layer(h, edge_attr, src, dst, p)
        return h
    edge_index = jnp.stack([src, dst])
    h = jnp.maximum(_layernorm(x, axis=-1), 0.0)
    x = x + _L0_gnn_ref(h, edge_attr_64, edge_index, L0_gnn_WQ, L0_gnn_WK, L0_gnn_WE, L0_gnn_WV, L0_gnn_WO, L0_gnn_bO, L0_gnn_ln1_g, L0_gnn_ln1_b, L0_gnn_W1, L0_gnn_b1, L0_gnn_W2, L0_gnn_b2, L0_gnn_ln2_g, L0_gnn_ln2_b)
    return x

_drawn_inputs = setup_inputs


def setup_inputs(seed=0):
    import zlib

    import numpy as np

    out = dict(_drawn_inputs(seed))
    spreads = {'L0_gnn_bO': (0.0, 0.1),
     'L0_gnn_ln1_g': (1.0, 0.2),
     'L0_gnn_ln1_b': (0.0, 0.1),
     'L0_gnn_b1': (0.0, 0.1),
     'L0_gnn_b2': (0.0, 0.1),
     'L0_gnn_ln2_g': (1.0, 0.2),
     'L0_gnn_ln2_b': (0.0, 0.1)}
    factors = {}
    for name, (base, spread) in spreads.items():
        noise = np.random.default_rng([zlib.crc32(name.encode()), seed]).standard_normal(out[name].shape)
        drawn = base * np.exp(spread * noise) if base else spread * noise
        out[name] = jnp.asarray(drawn.astype(out[name].dtype))
    for name, factor in factors.items():
        out[name] = (out[name] * factor).astype(out[name].dtype)
    return out
```

```python
from contextlib import ExitStack

import numpy as np
import concourse.bass as bass
from concourse import mybir

F32 = mybir.dt.float32
BF16 = mybir.dt.bfloat16
I32 = mybir.dt.int32
ALU = mybir.AluOpType
ACT = mybir.ActivationFunctionType
X = mybir.AxisListType.X

P = 128
N, E, D, H, L = 12500, 200000, 64, 4, 2
DH = D // H
HID = 2 * D
EPS = 1e-5
TILES = 8
RING = 4
PAIR = 2
GE = TILES * P
ITERS = -(-E // (RING * GE))
GROUPS = ITERS * RING
EDGE_TILES = GROUPS * TILES
EP = GROUPS * GE
WINDOWS = PAIR * ITERS
NP_ = WINDOWS * P
assert NP_ >= N and GROUPS % 2 == 0
LAG = 2
Q_ROWS = NP_ + P
DUMP = NP_ + P
S_ROWS = NP_ + 2 * P
SW = D + H
CREDIT = 4
NEWTON = 3
RSQRT_MAGIC = float(0x5F3759DF)
IDX_AHEAD = 3


def done(n):
    return n + (CREDIT + 1)


def gnn(nc, x, src, dst, base, edge_attr_t, wkvq, we, wo, bo, g1, be1, w1, b1, w2, b2, g2, be2, out):
    ctx = ExitStack()
    with ctx:
        def sb(name, shape, dt=F32):
            return ctx.enter_context(nc.sbuf_tensor(name, shape, dt))

        def bank(name, shape, dt=F32):
            return ctx.enter_context(nc.psum_tensor(name, shape, dt))

        def sem(name):
            return ctx.enter_context(nc.semaphore(name))

        kv_table = [nc.dram_tensor(f"kv_table{l}", (NP_, 2 * D), F32).ap() for l in range(L)]
        q_table = [nc.dram_tensor(f"q_table{l}", (Q_ROWS, 3 * D), BF16).ap() for l in range(L)]
        sums = [nc.dram_tensor(f"sums{l}", (S_ROWS, SW), F32).ap() for l in range(L)]

        x_all = sb("x_all", [P, WINDOWS, D])
        h_all = sb("h_all", [P, WINDOWS, D])
        src_all = sb("src_all", [P, (GROUPS + IDX_AHEAD) * TILES], I32)
        dst_all = sb("dst_all", [P, EDGE_TILES], I32)
        base_all = sb("base_all", [P, GROUPS], I32)
        rel = sb("rel", [P, GROUPS + 1, TILES + 1])
        src_slot = sb("src_slot", [P, RING, TILES], I32)
        kv = sb("kv", [P, RING, TILES, 2 * D])
        attr = sb("attr", [D, RING, GE])
        q_win = sb("q_win", [P, 2, 3 * D], BF16)
        onehot = sb("onehot", [P, 2, TILES + 1, P], BF16)
        onehot_f = sb("onehot_f", [P, 2, TILES + 1, P])
        onehot_t = sb("onehot_t", [P, 2, TILES, P], BF16)
        prod = sb("prod", [P, TILES, D])
        logit = sb("logit", [P, TILES * H])
        clip = sb("clip", [P, TILES * H])
        msg = sb("msg", [P, 2, TILES + 1, SW])
        nsum = sb("nsum", [P, PAIR, SW])
        zrec = sb("zrec", [P, PAIR, H])
        attn = sb("attn", [P, PAIR, D])
        attn_t = sb("attn_t", [D + 1, PAIR * P])
        res = sb("res", [P, PAIR, D])
        cen = sb("cen", [P, PAIR, D])
        sq = sb("sq", [P, PAIR, D])
        tot = sb("tot", [P, PAIR])
        ssq = sb("ssq", [P, PAIR])
        rstd = sb("rstd", [P, PAIR])
        half = sb("half", [P, PAIR])
        bits = sb("bits", [P, PAIR], I32)
        h1 = sb("h1", [P, PAIR, D])
        h1_t = sb("h1_t", [D, PAIR * P])
        hid = sb("hid", [HID, PAIR * P])
        h2 = sb("h2", [P, PAIR, D])
        h2_t = sb("h2_t", [D, PAIR * P])
        kvq = sb("kvq", [P, PAIR, 3 * D])
        q_rest = sb("q_rest", [P, PAIR, D])
        q_split = sb("q_split", [P, PAIR, 3 * D], BF16)
        CH = 14
        assert WINDOWS % CH == 0
        c_cen = sb("c_cen", [P, CH, D])
        c_sq = sb("c_sq", [P, CH, D])
        c_tot = sb("c_tot", [P, CH])
        c_ssq = sb("c_ssq", [P, CH])
        c_rstd = sb("c_rstd", [P, CH])
        c_half = sb("c_half", [P, CH])
        c_bits = sb("c_bits", [P, CH], I32)
        wkvq_sb = sb("wkvq_sb", [D, L, 3 * D])
        we_sb = sb("we_sb", [D, L, D])
        wo_sb = sb("wo_sb", [D + 1, L, D])
        w1_sb = sb("w1_sb", [D, L, HID])
        b1_sb = sb("b1_sb", [HID, L])
        w2_sb = sb("w2_sb", [HID, L, D])
        b2_sb = sb("b2_sb", [1, L, D])
        norm_sb = sb("norm_sb", [P, L, 4, D])
        ones = sb("ones", [P, P])
        ident = sb("ident", [P, P])
        ident_b = sb("ident_b", [P, P], BF16)
        iota_i = sb("iota_i", [P, P], I32)
        part_i = sb("part_i", [P, 1], I32)
        iota_f = sb("iota_f", [P, P])
        part_f = sb("part_f", [P, 1])
        dump_f = sb("dump_f", [P, 1])
        below = sb("below", [P, P])
        zeros = sb("zeros", [P, S_ROWS // P * SW // 4])
        chk = sb("chk", [P, 8])
        step_f = sb("step_f", [P, GROUPS])
        base_f = sb("base_f", [P, GROUPS])
        limit_i = sb("limit_i", [P, ITERS - LAG], I32)
        limit_f = sb("limit_f", [P, ITERS - LAG])
        dst_f = sb("dst_f", [P, EDGE_TILES])
        flag = sb("flag", [1, 1], I32)
        g_src = sb("g_src", [P, 1], I32)
        g_dst = sb("g_dst", [P, 1], I32)
        g_to = sb("g_to", [P, 1], I32)
        g_dstf = sb("g_dstf", [P, 1])
        g_kv = sb("g_kv", [P, 2 * D])
        g_q3 = sb("g_q3", [P, 3 * D], BF16)
        g_q = sb("g_q", [P, D])
        g_attr = sb("g_attr", [D, P])
        g_dup = sb("g_dup", [P, 4])
        g_bc = sb("g_bc", [P, P])
        g_same = sb("g_same", [P, P])
        g_tmp = sb("g_tmp", [P, P])
        g_msg = sb("g_msg", [P, SW])
        g_sum = sb("g_sum", [P, SW])

        e_bank = bank("e_bank", [P, TILES, D])
        q_bank = bank("q_bank", [P, TILES, D])
        t_bank = bank("t_bank", [P, TILES, P], BF16)
        acc_bank = bank("acc_bank", [P, 512])
        nt_bank = bank("nt_bank", [P, 512])
        hid_bank = bank("hid_bank", [P, 512])
        no_bank = bank("no_bank", [P, 512])
        iota_bank = bank("iota_bank", [P, 512])
        acc = acc_bank[:, 0:SW]
        iota_ps = iota_bank[:, 0:P]

        weights_loaded = sem("weights_loaded")
        wo_loaded = sem("wo_loaded")
        x_loaded = sem("x_loaded")
        indices_loaded = sem("indices_loaded")
        attr_loaded = [sem(f"attr_loaded{s}") for s in range(RING)]
        q_win_loaded = [sem(f"q_win_loaded{s}") for s in range(2)]
        kv_gathered = [sem(f"kv_gathered{s}") for s in range(RING)]
        q_pad_zeroed = sem("q_pad_zeroed")
        sums_written = sem("sums_written")
        nsum_loaded = sem("nsum_loaded")
        kv_stored = sem("kv_stored")
        q_stored = sem("q_stored")
        out_stored = sem("out_stored")
        pool_consts = sem("pool_consts")
        dve_consts = sem("dve_consts")
        h0_ready = sem("h0_ready")
        h0_step = sem("h0_step")
        chk_step = sem("chk_step")
        bad_ready = sem("bad_ready")
        bad_summed = sem("bad_summed")
        flag_ready = sem("flag_ready")
        src_staged = sem("src_staged")
        onehot_built = sem("onehot_built")
        onehot_cast = sem("onehot_cast")
        onehot_turned = sem("onehot_turned")
        onehot_t_ready = sem("onehot_t_ready")
        edge_projected = sem("edge_projected")
        query_spread = sem("query_spread")
        key_used = sem("key_used")
        query_used = sem("query_used")
        logit_ready = sem("logit_ready")
        clip_ready = sem("clip_ready")
        score_ready = sem("score_ready")
        msg_ready = sem("msg_ready")
        group_summed = sem("group_summed")
        carry_ready = sem("carry_ready")
        attn_ready = sem("attn_ready")
        attn_turned = sem("attn_turned")
        attn_t_ready = sem("attn_t_ready")
        attn_projected = sem("attn_projected")
        h1_ready = sem("h1_ready")
        h1_turned = sem("h1_turned")
        h1_t_ready = sem("h1_t_ready")
        hid_ready = sem("hid_ready")
        relu_ready = sem("relu_ready")
        ffn_ready = sem("ffn_ready")
        h2_ready = sem("h2_ready")
        h2_turned = sem("h2_turned")
        h2_t_ready = sem("h2_t_ready")
        kvq_projected = sem("kvq_projected")
        kvq_staged = sem("kvq_staged")
        q_split_ready = sem("q_split_ready")
        node_step = sem("node_step")
        split_step = sem("split_step")
        sp_passed = sem("sp_passed")
        pool_passed = sem("pool_passed")
        pe_passed = sem("pe_passed")
        g_indexed = sem("g_indexed")
        g_attr_loaded = sem("g_attr_loaded")
        g_gathered = sem("g_gathered")
        g_step = sem("g_step")
        g_projected = sem("g_projected")
        g_clipped = sem("g_clipped")
        g_scored = sem("g_scored")
        g_msg_ready = sem("g_msg_ready")
        g_summed = sem("g_summed")
        g_sum_ready = sem("g_sum_ready")
        g_added = sem("g_added")

        ZERO_FILLS = 4 * L
        NORM_STEPS = 4 + 4 + 3 * NEWTON + 2
        NODE_STEPS = 5 + 2 * NORM_STEPS
        SPLIT_STEPS = 3
        G_STEPS = 11
        block = ctx.enter_context(nc.Block())

        def window_rows(table, j):
            return table[bass.ds(j * (PAIR * P), PAIR * P), :].rearrange("(w p) c -> p w c", p=P)

        @block.sync
        def _(sp):
            sp.dma_start(x_all[:], x).then_inc(x_loaded, 16)
            sp.dma_start(src_all[:], src).then_inc(indices_loaded, 16)
            sp.dma_start(dst_all[:], dst).then_inc(indices_loaded, 16)
            sp.dma_start(base_all[:], base.partition_broadcast(P)).then_inc(indices_loaded, 16)
            sp.dma_start(wkvq_sb[:], wkvq.rearrange("l k n -> k l n")).then_inc(weights_loaded, 16)
            sp.dma_start(we_sb[:], we.rearrange("l k n -> k l n")).then_inc(weights_loaded, 16)
            sp.dma_start(wo_sb[0:D], wo.rearrange("l k n -> k l n")).then_inc(weights_loaded, 16)
            sp.dma_start(wo_sb[D:D + 1], bo.unsqueeze(0)).then_inc(weights_loaded, 16)
            sp.dma_start(w1_sb[:], w1.rearrange("l k n -> k l n")).then_inc(weights_loaded, 16)
            sp.dma_start(b1_sb[:], b1).then_inc(weights_loaded, 16)
            sp.dma_start(w2_sb[:], w2.rearrange("l k n -> k l n")).then_inc(weights_loaded, 16)
            sp.dma_start(b2_sb[:], b2.unsqueeze(0)).then_inc(weights_loaded, 16)
            for k, a in enumerate((g1, be1, g2, be2)):
                sp.dma_start(norm_sb[:, :, k, :], a.partition_broadcast(P)).then_inc(weights_loaded, 16)
            sp.wait_ge(pool_consts, 1)
            part = S_ROWS // 4
            for l in range(L):
                for k in range(4):
                    sp.dma_start(sums[l][k * part:(k + 1) * part, :].rearrange("(p r) c -> p (r c)", p=P),
                                 zeros[:]).then_inc(sums_written, 16)
                sp.dma_start(q_table[l][NP_:Q_ROWS, :], zeros[:, 0:3 * D // 2].bitcast(BF16)).then_inc(q_pad_zeroed, 16)
            sp.wait_ge(q_pad_zeroed, 16 * L)
            sp.wait_ge(indices_loaded, 48)

            def load_group(l, i, s):
                n = l * GROUPS + 4 * i + s
                sp.wait_ge(edge_projected, done(n - RING))
                sp.dma_start(attr[:, s, :], edge_attr_t[:, bass.ds((4 * i + s) * GE, GE)]).then_inc(attr_loaded[s], 16)
                first = sp.value_load(base_all[0:1, bass.ds(4 * i + s, 1)], min_val=0, max_val=NP_ - 1)
                sp.wait_ge(query_spread, done(n - 2))
                sp.dma_start(q_win[:, s % 2, :], q_table[l][bass.ds(first, P), :]).then_inc(q_win_loaded[s % 2], 16)

            def load_nsum(l, j, written):
                sp.wait_ge(sums_written, written)
                sp.sem_inc(sp_passed, 1)
                sp.wait_ge(attn_ready, done(l * ITERS + j - 1))
                sp.dma_start(nsum[:], window_rows(sums[l], j)).then_inc(nsum_loaded, 16)

            sp.wait_ge(flag_ready, 1)
            bad = sp.value_load(flag[0:1, 0:1], min_val=0, max_val=P)
            with sp.If(bad < 1):
                for l in range(L):
                    sp.wait_ge(q_stored, 16 * ITERS * (l + 1))
                    with sp.Fori(0, LAG) as i:
                        for s in range(RING):
                            load_group(l, i, s)
                    with sp.Fori(LAG, ITERS) as i:
                        for s in range(RING):
                            load_group(l, i, s)
                            if s == 0:
                                load_nsum(l, i - LAG, 16 * (ZERO_FILLS + l * GROUPS) + 16 * (4 * i - 2))
                    with sp.Fori(ITERS, ITERS + LAG) as i:
                        load_nsum(l, i - LAG, 16 * (ZERO_FILLS + (l + 1) * GROUPS))
            with sp.Else():
                for l in range(L):
                    with sp.Fori(0, EDGE_TILES) as t:
                        sp.dma_start(g_attr[:], edge_attr_t[:, bass.ds(t * P, P)]).then_inc(g_attr_loaded, 16)
                        sp.wait_ge(g_projected, l * EDGE_TILES + t + 1)
                        sp.sem_inc(sp_passed, 1)
                    sp.wait_ge(g_added, 16 * EDGE_TILES * (l + 1))
                    with sp.Fori(0, ITERS) as j:
                        load_nsum(l, j, 16 * ZERO_FILLS)

        @block.gpsimd
        def _(pool):
            nc.gpsimd.memset(zeros[:], 0.0).then_inc(pool_consts, 1)
            nc.gpsimd.memset(ones[:], 1.0).then_inc(pool_consts, 1)
            nc.gpsimd.memset(msg[:], 0.0).then_inc(pool_consts, 1)
            nc.gpsimd.memset(attn_t[:], 1.0).then_inc(pool_consts, 1)
            nc.gpsimd.iota(iota_i[:], [[1, P]], base=0, channel_multiplier=0).then_inc(pool_consts, 1)
            nc.gpsimd.iota(part_i[:], [[0, 1]], base=0, channel_multiplier=1).then_inc(pool_consts, 1)
            nc.gpsimd.iota(limit_i[:], [[PAIR * P, ITERS - LAG]], base=PAIR * P, channel_multiplier=0)\
                .then_inc(pool_consts, 1)

            pool.wait_ge(flag_ready, 1)
            bad = pool.value_load(flag[0:1, 0:1], min_val=0, max_val=P)
            with pool.If(bad < 1):
                for l in range(L):
                    pool.wait_ge(kv_stored, 16 * ITERS * (l + 1))
                    with pool.Fori(0, ITERS) as i:
                        for s in range(RING):
                            n = l * GROUPS + 4 * i + s
                            pool.wait_ge(src_staged, done(n))
                            pool.wait_ge(msg_ready, done(n - RING))
                            pool.sem_inc(pool_passed, 1)
                            for t in range(TILES):
                                nc.gpsimd.indirect_dma_start(
                                    out=kv[:, s, t, :], out_offset=None, in_=kv_table[l][:, :],
                                    in_offset=bass.IndirectOffsetOnAxis(ap=src_slot[:, s, t:t + 1], axis=0),
                                ).then_inc(kv_gathered[s], 16)
            with pool.Else():
                for l in range(L):
                    pool.wait_ge(q_stored, 16 * ITERS * (l + 1))
                    pool.wait_ge(kv_stored, 16 * ITERS * (l + 1))
                    pool.wait_ge(q_pad_zeroed, 16 * L)
                    pool.wait_ge(sums_written, 16 * ZERO_FILLS)
                    with pool.Fori(0, EDGE_TILES) as t:
                        n = l * EDGE_TILES + t
                        pool.wait_ge(g_indexed, n + 1)
                        pool.sem_inc(pool_passed, 1)
                        nc.gpsimd.indirect_dma_start(
                            out=g_kv[:], out_offset=None, in_=kv_table[l][:, :],
                            in_offset=bass.IndirectOffsetOnAxis(ap=g_src[:, 0:1], axis=0)).then_inc(g_gathered, 16)
                        nc.gpsimd.indirect_dma_start(
                            out=g_q3[:], out_offset=None, in_=q_table[l][:, :],
                            in_offset=bass.IndirectOffsetOnAxis(ap=g_dst[:, 0:1], axis=0)).then_inc(g_gathered, 16)
                        pool.wait_ge(g_sum_ready, n + 1)
                        pool.sem_inc(pool_passed, 1)
                        nc.gpsimd.indirect_dma_start(
                            out=sums[l][:, :], out_offset=bass.IndirectOffsetOnAxis(ap=g_to[:, 0:1], axis=0),
                            in_=g_sum[:], in_offset=None, compute_op=ALU.add).then_inc(g_added, 16)
                        pool.wait_ge(g_added, 16 * (n + 1))
                        pool.sem_inc(pool_passed, 1)

        @block.tensor
        def _(pe):
            for done_by_pe in (onehot_turned, edge_projected, query_spread, group_summed, attn_turned,
                               attn_projected, h1_turned, hid_ready, ffn_ready, h2_turned, kvq_projected):
                pe.sem_inc(done_by_pe, CREDIT)

            def turn_attn(m):
                pe.wait_ge(attn_ready, done(m))
                pe.sem_inc(pe_passed, 1)
                for w in range(PAIR):
                    last = pe.transpose(nt_bank[0:D, w * P:(w + 1) * P], attn[:, w, :], ident[:])
                last.then_inc(attn_turned, 1)

            def project_attn(l, m):
                pe.wait_ge(attn_t_ready, done(m))
                for w in range(PAIR):
                    last = pe.matmul(no_bank[:, w * D:(w + 1) * D], attn_t[:, w * P:(w + 1) * P], wo_sb[:, l, :],
                                     start=True, stop=True)
                last.then_inc(attn_projected, 1)

            def turn_h1(m):
                pe.wait_ge(h1_ready, done(m))
                pe.sem_inc(pe_passed, 1)
                for w in range(PAIR):
                    last = pe.transpose(nt_bank[0:D, w * P:(w + 1) * P], h1[:, w, :], ident[:])
                last.then_inc(h1_turned, 1)

            def project_hidden(l, m):
                pe.wait_ge(h1_t_ready, done(m))
                pe.matmul(hid_bank[:, 0:PAIR * P], w1_sb[:, l, :], h1_t[:], start=True, stop=True).then_inc(hid_ready, 1)

            def project_ffn(l, m):
                pe.wait_ge(relu_ready, done(m))
                for w in range(PAIR):
                    o = no_bank[:, w * D:(w + 1) * D]
                    pe.matmul(o, hid[:, w * P:(w + 1) * P], w2_sb[:, l, :], start=True, stop=False)
                    last = pe.matmul(o, ones[0:1, :], b2_sb[:, l, :], start=False, stop=True)
                last.then_inc(ffn_ready, 1)

            def turn_h2(b):
                pe.wait_ge(h2_ready, done(b))
                pe.sem_inc(pe_passed, 1)
                for w in range(PAIR):
                    last = pe.transpose(nt_bank[0:D, w * P:(w + 1) * P], h2[:, w, :], ident[:])
                last.then_inc(h2_turned, 1)

            def project_kvq(l, b):
                pe.wait_ge(h2_t_ready, done(b))
                pe.wait_ge(kvq_staged, done(b - 1))
                for w in range(PAIR):
                    last = pe.matmul(no_bank[:, w * 3 * D:(w + 1) * 3 * D], h2_t[:, w * P:(w + 1) * P],
                                     wkvq_sb[:, l, :], start=True, stop=True)
                last.then_inc(kvq_projected, 1)

            def turn_onehot(s, n):
                pe.wait_ge(onehot_built, done(n))
                pe.wait_ge(onehot_t_ready, done(n - 1))
                for t in range(TILES):
                    last = pe.transpose(t_bank[:, t, :], onehot[:, s % 2, t, :], ident_b[:])
                last.then_inc(onehot_turned, 1)

            def project_edges(l, i, s, n):
                pe.wait_ge(attr_loaded[s], 16 * (l * ITERS + i + 1))
                pe.wait_ge(key_used, done(n - 1))
                for t in range(TILES):
                    last = pe.matmul(e_bank[:, t, :], attr[:, s, t * P:(t + 1) * P], we_sb[:, l, :],
                                     start=True, stop=True)
                last.then_inc(edge_projected, 1)

            def spread_query(l, i, s, n):
                pe.wait_ge(onehot_t_ready, done(n))
                pe.wait_ge(q_win_loaded[s % 2], 16 * (2 * (l * ITERS + i) + s // 2 + 1))
                pe.wait_ge(query_used, done(n - 1))
                for t in range(TILES):
                    for k in range(3):
                        last = pe.matmul(q_bank[:, t, :], onehot_t[:, s % 2, t, :], q_win[:, s % 2, k * D:(k + 1) * D],
                                         start=(k == 0), stop=(k == 2))
                last.then_inc(query_spread, 1)

            def sum_group(s, n):
                pe.wait_ge(msg_ready, done(n))
                pe.wait_ge(onehot_cast, done(n))
                pe.wait_ge(carry_ready, done(n - 1))
                for t in range(TILES + 1):
                    last = pe.matmul(acc, onehot_f[:, s % 2, t, :], msg[:, s % 2, t, :],
                                     start=(t == 0), stop=(t == TILES))
                last.then_inc(group_summed, 1)

            pe.wait_ge(weights_loaded, 16 * 12)
            pe.wait_ge(dve_consts, 4)
            with pe.Fori(0, ITERS) as j:
                pe.wait_ge(h2_t_ready, done(j - 1))
                turn_h2(j)
                project_kvq(0, j)

            pe.wait_ge(bad_ready, 1)
            pe.matmul(nt_bank[0:1, 0:1], chk[:, 7:8], ones[:, 0:1], start=True, stop=True).then_inc(bad_summed, 1)
            pe.wait_ge(flag_ready, 1)
            bad = pe.value_load(flag[0:1, 0:1], min_val=0, max_val=P)
            with pe.If(bad < 1):
                turn_onehot(0, 0)
                for l in range(L):
                    def one_pass(i, edges, nodes):
                        m = l * ITERS + i - LAG
                        for s in range(RING):
                            n = l * GROUPS + 4 * i + s
                            if edges:
                                project_edges(l, i, s, n)
                                spread_query(l, i, s, n)
                                turn_onehot(s + 1, n + 1)
                            if nodes and s == 1:
                                turn_attn(m)
                            if nodes and s == 2:
                                turn_h1(m)
                            if nodes and s == 3:
                                project_ffn(l, m)
                            if edges:
                                sum_group(s, n)
                            if nodes and s == 1:
                                project_attn(l, m)
                            if nodes and s == 2:
                                project_hidden(l, m)
                            if nodes and s == 3 and l + 1 < L:
                                turn_h2(m + ITERS)
                                project_kvq(l + 1, m + ITERS)
                    with pe.Fori(0, LAG) as i:
                        one_pass(i, True, False)
                    with pe.Fori(LAG, ITERS) as i:
                        one_pass(i, True, True)
                    with pe.Fori(ITERS, ITERS + LAG) as i:
                        one_pass(i, False, True)
            with pe.Else():
                for l in range(L):
                    with pe.Fori(0, EDGE_TILES) as t:
                        n = l * EDGE_TILES + t
                        pe.wait_ge(g_attr_loaded, 16 * (n + 1))
                        pe.wait_ge(g_indexed, n + 1)
                        pe.matmul(e_bank[:, 0, :], g_attr[:], we_sb[:, l, :], start=True, stop=True)
                        pe.transpose(acc_bank[:, 0:P], g_bc[:], ident[:]).then_inc(g_projected, 1)
                        pe.wait_ge(g_msg_ready, n + 1)
                        pe.matmul(q_bank[:].rearrange("p t d -> p (t d)")[:, 0:SW], g_same[:], g_msg[:],
                                  start=True, stop=True).then_inc(g_summed, 1)
                    with pe.Fori(0, ITERS) as j:
                        m = l * ITERS + j
                        turn_attn(m)
                        project_attn(l, m)
                        turn_h1(m)
                        project_hidden(l, m)
                        project_ffn(l, m)
                        if l + 1 < L:
                            turn_h2(m + ITERS)
                            project_kvq(l + 1, m + ITERS)

        @block.scalar
        def _(act):
            for done_by_act in (onehot_cast, onehot_t_ready, score_ready, carry_ready, attn_t_ready, h1_t_ready,
                                relu_ready, h2_t_ready, kvq_staged):
                act.sem_inc(done_by_act, CREDIT)

            def copy_attn_t(m):
                act.wait_ge(attn_turned, done(m))
                nc.scalar.copy(attn_t[0:D, :], nt_bank[0:D, 0:PAIR * P]).then_inc(attn_t_ready, 1)

            def copy_h1_t(m):
                act.wait_ge(h1_turned, done(m))
                nc.scalar.copy(h1_t[:], nt_bank[0:D, 0:PAIR * P]).then_inc(h1_t_ready, 1)

            def relu_hidden(l, m):
                act.wait_ge(hid_ready, done(m))
                nc.scalar.activation(hid[:], hid_bank[:, 0:PAIR * P], ACT.Relu, bias=b1_sb[:, l:l + 1])\
                    .then_inc(relu_ready, 1)

            def copy_h2_t(b):
                act.wait_ge(h2_turned, done(b))
                nc.scalar.copy(h2_t[:], nt_bank[0:D, 0:PAIR * P]).then_inc(h2_t_ready, 1)

            def store_kv(l, j, b, first=False):
                act.wait_ge(kvq_projected, done(b))
                act.wait_ge(q_split_ready, done(b - 1))
                if not first:
                    act.wait_ge(kv_stored, 16 * b)
                nc.scalar.copy(kvq[:].rearrange("p w c -> p (w c)"), no_bank[:, 0:PAIR * 3 * D]).then_inc(kvq_staged, 1)
                act.wait_ge(kvq_staged, done(b))
                act.dma_start(window_rows(kv_table[l], j), kvq[:, :, 0:2 * D]).then_inc(kv_stored, 16)

            def store_q(l, j, b):
                act.wait_ge(q_split_ready, done(b))
                act.dma_start(window_rows(q_table[l], j), q_split[:]).then_inc(q_stored, 16)

            def cast_onehot(s, n):
                act.wait_ge(onehot_built, done(n))
                nc.scalar.copy(onehot_f[:, s % 2], onehot[:, s % 2]).then_inc(onehot_cast, 1)

            def copy_onehot_t(s, n):
                act.wait_ge(onehot_turned, done(n))
                nc.scalar.copy(onehot_t[:, s % 2], t_bank[:]).then_inc(onehot_t_ready, 1)

            def exp_scores(s, n):
                act.wait_ge(clip_ready, done(n))
                nc.scalar.activation(msg[:, s % 2, 0:TILES, D:SW], clip[:].rearrange("p (t h) -> p t h", h=H), ACT.Exp,
                                     scale=DH ** -0.5).then_inc(score_ready, 1)

            def write_sums(l, i, s, n):
                act.wait_ge(group_summed, done(n))
                nc.scalar.copy(msg[:, (s + 1) % 2, TILES, :], acc).then_inc(carry_ready, 1)
                first = act.value_load(base_all[0:1, bass.ds(4 * i + s, 1)], min_val=0, max_val=NP_ - 1)
                act.wait_ge(sums_written, 16 * ZERO_FILLS + 16 * n)
                act.wait_ge(carry_ready, done(n))
                act.dma_start(sums[l][bass.ds(first, P), :], msg[:, (s + 1) % 2, TILES, :]).then_inc(sums_written, 16)

            copy_h2_t(0)
            store_kv(0, 0, 0, first=True)
            store_q(0, 0, 0)
            with act.Fori(1, ITERS) as j:
                copy_h2_t(j)
                store_kv(0, j, j)
                store_q(0, j, j)

            act.wait_ge(flag_ready, 1)
            bad = act.value_load(flag[0:1, 0:1], min_val=0, max_val=P)
            with act.If(bad < 1):
                cast_onehot(0, 0)
                copy_onehot_t(0, 0)
                for l in range(L):
                    def one_pass(i, edges, nodes):
                        m = l * ITERS + i - LAG
                        for s in range(RING):
                            n = l * GROUPS + 4 * i + s
                            if edges:
                                cast_onehot(s + 1, n + 1)
                                copy_onehot_t(s + 1, n + 1)
                            if nodes and s == 1:
                                copy_attn_t(m)
                            if nodes and s == 2:
                                copy_h1_t(m)
                            if edges:
                                exp_scores(s, n)
                                write_sums(l, i, s, n)
                            if nodes and s == 2:
                                relu_hidden(l, m)
                            if nodes and s == 3:
                                if l + 1 < L:
                                    copy_h2_t(m + ITERS)
                                    store_kv(l + 1, i - LAG, m + ITERS)
                                    store_q(l + 1, i - LAG, m + ITERS)
                                else:
                                    store_out(i - LAG, m)

                    def store_out(j, m):
                        act.wait_ge(h2_ready, done(m + ITERS))
                        act.dma_start(out[:, bass.ds(j * PAIR, PAIR), :], x_all[:, bass.ds(j * PAIR, PAIR), :])\
                            .then_inc(out_stored, 16)

                    with act.Fori(0, LAG) as i:
                        one_pass(i, True, False)
                    with act.Fori(LAG, ITERS) as i:
                        one_pass(i, True, True)
                    with act.Fori(ITERS, ITERS + LAG) as i:
                        one_pass(i, False, True)
                act.wait_ge(sums_written, 16 * (ZERO_FILLS + L * GROUPS))
            with act.Else():
                for l in range(L):
                    with act.Fori(0, EDGE_TILES) as t:
                        n = l * EDGE_TILES + t
                        act.wait_ge(g_clipped, n + 1)
                        nc.scalar.activation(g_msg[:, D:SW], clip[:, 0:H], ACT.Exp, scale=DH ** -0.5).then_inc(g_scored, 1)
                    with act.Fori(0, ITERS) as j:
                        m = l * ITERS + j
                        copy_attn_t(m)
                        copy_h1_t(m)
                        relu_hidden(l, m)
                        if l + 1 < L:
                            copy_h2_t(m + ITERS)
                            store_kv(l + 1, j, m + ITERS)
                            store_q(l + 1, j, m + ITERS)
                        else:
                            act.wait_ge(h2_ready, done(m + ITERS))
                            act.dma_start(out[:, bass.ds(j * PAIR, PAIR), :], x_all[:, bass.ds(j * PAIR, PAIR), :])\
                                .then_inc(out_stored, 16)
            act.wait_ge(out_stored, 16 * ITERS)
            act.wait_ge(kv_stored, 16 * L * ITERS)
            act.wait_ge(q_stored, 16 * L * ITERS)

        @block.vector
        def _(dve):
            v = nc.vector
            for done_by_dve in (src_staged, onehot_built, key_used, query_used, logit_ready, clip_ready, msg_ready,
                                attn_ready, h1_ready, h2_ready, q_split_ready, node_step, split_step):
                dve.sem_inc(done_by_dve, CREDIT)

            def pairs(a):
                return a.unsqueeze(2).to_broadcast([P, PAIR, D])

            dve.wait_ge(pool_consts, 7)
            v.tensor_copy(iota_f[:], iota_i[:]).then_inc(chk_step, 1)
            v.tensor_copy(part_f[:], part_i[:]).then_inc(chk_step, 1)
            dve.wait_ge(chk_step, 2)
            v.tensor_copy(iota_ps, iota_f[:]).then_inc(dve_consts, 1)
            v.tensor_scalar(ident[:], iota_f[:], part_f[:, 0:1], None, ALU.is_equal).then_inc(dve_consts, 1)
            v.tensor_scalar(ident_b[:], iota_f[:], part_f[:, 0:1], None, ALU.is_equal).then_inc(dve_consts, 1)
            v.tensor_scalar(below[:], iota_f[:], part_f[:, 0:1], None, ALU.is_lt).then_inc(dve_consts, 1)
            v.tensor_scalar(dump_f[:], part_f[:], float(DUMP), None, ALU.add).then_inc(chk_step, 1)

            def rsqrt(y, ssq, half, bits):
                yield v.tensor_scalar(ssq[:], ssq[:], 1.0 / D, EPS, ALU.mult, ALU.add)
                yield v.tensor_scalar(bits[:], ssq[:].bitcast(I32), 1, None, ALU.logical_shift_right)
                yield v.tensor_scalar(y[:].bitcast(I32), bits[:], -1.0, RSQRT_MAGIC, ALU.mult, ALU.add)
                yield v.tensor_scalar(half[:], ssq[:], -0.5, None, ALU.mult)
                for _ in range(NEWTON):
                    yield v.tensor_tensor(ssq[:], y[:], y[:], ALU.mult)
                    yield v.tensor_tensor(ssq[:], ssq[:], half[:], ALU.mult)
                    yield v.scalar_tensor_tensor(y[:], ssq[:], 1.5, y[:], ALU.add, ALU.mult)

            dve.wait_ge(x_loaded, 16)
            steps = [0]

            def h0_link(ins):
                steps[0] += 1
                ins.then_inc(h0_step, 1)
                dve.wait_ge(h0_step, steps[0])

            def chunk(a):
                return a.unsqueeze(2).to_broadcast([P, CH, D])

            for c in range(WINDOWS // CH):
                xc = x_all[:, c * CH:(c + 1) * CH, :]
                h0_link(v.tensor_reduce(c_tot[:], xc, X, ALU.add))
                h0_link(v.scalar_tensor_tensor(c_cen[:], chunk(c_tot[:]), -1.0 / D, xc, ALU.mult, ALU.add))
                h0_link(v.tensor_tensor(c_sq[:], c_cen[:], c_cen[:], ALU.mult))
                h0_link(v.tensor_reduce(c_ssq[:], c_sq[:], X, ALU.add))
                for ins in rsqrt(c_rstd, c_ssq, c_half, c_bits):
                    h0_link(ins)
                h0_link(v.tensor_tensor(c_sq[:], c_cen[:], chunk(c_rstd[:]), ALU.mult))
                v.tensor_scalar(h_all[:, c * CH:(c + 1) * CH, :], c_sq[:], 0.0, None, ALU.max).then_inc(h0_ready, 1)
                dve.wait_ge(h0_ready, c + 1)

            cs = [3]

            def chk_link(ins):
                cs[0] += 1
                ins.then_inc(chk_step, 1)
                dve.wait_ge(chk_step, cs[0])

            dve.wait_ge(indices_loaded, 48)
            chk_link(v.tensor_copy(dst_f[:], dst_all[:]))
            chk_link(v.tensor_copy(base_f[:], base_all[:]))
            chk_link(v.tensor_copy(limit_f[:], limit_i[:]))
            chk_link(v.tensor_tensor(rel[:, 0:GROUPS, 0:TILES], dst_f[:].rearrange("p (g t) -> p g t", t=TILES),
                                     base_f[:].unsqueeze(2).to_broadcast([P, GROUPS, TILES]), ALU.subtract))
            chk_link(v.tensor_tensor(step_f[:, 1:GROUPS], base_f[:, 1:GROUPS], base_f[:, 0:GROUPS - 1], ALU.subtract))
            chk_link(v.memset(rel[:, 0, TILES:TILES + 1], -1.0))
            chk_link(v.tensor_scalar(rel[:, 1:GROUPS, TILES], step_f[:, 1:GROUPS], part_f[:, 0:1], -1.0,
                                     ALU.subtract, ALU.mult))
            chk_link(v.tensor_copy(rel[:, GROUPS, :], rel[:, 0, :]))
            chk_link(v.tensor_reduce(chk[:, 0:1], rel[:, 0:GROUPS, 0:TILES], mybir.AxisListType.XY, ALU.min))
            chk_link(v.tensor_reduce(chk[:, 3:4], rel[:, 0:GROUPS, 0:TILES], mybir.AxisListType.XY, ALU.max))
            chk_link(v.tensor_reduce(chk[:, 1:2], step_f[:, 1:GROUPS], X, ALU.min))
            chk_link(v.tensor_tensor(limit_f[:], base_f[:, 6:6 + 4 * (ITERS - LAG - 1) + 1:4], limit_f[:], ALU.subtract))
            chk_link(v.tensor_reduce(chk[:, 2:3], limit_f[:], X, ALU.min))
            chk_link(v.tensor_scalar(chk[:, 3:4], chk[:, 3:4], -1.0, float(P - 1), ALU.mult, ALU.add))
            chk_link(v.tensor_reduce(chk[:, 6:7], chk[:, 0:4], X, ALU.min))
            v.tensor_scalar(chk[:, 7:8], chk[:, 6:7], 0.0, None, ALU.is_lt).then_inc(bad_ready, 1)
            dve.wait_ge(weights_loaded, 16 * 12)

            def link(m, k, ins):
                ins.then_inc(node_step, 1)
                dve.wait_ge(node_step, m * NODE_STEPS + (k + CREDIT + 1))

            def norm(m, k, y, g, b, last, ready):
                link(m, k, v.tensor_reduce(tot[:], y, X, ALU.add))
                link(m, k + 1, v.scalar_tensor_tensor(cen[:], pairs(tot[:]), -1.0 / D, y, ALU.mult, ALU.add))
                link(m, k + 2, v.tensor_tensor(sq[:], cen[:], cen[:], ALU.mult))
                link(m, k + 3, v.tensor_reduce(ssq[:], sq[:], X, ALU.add))
                k += 4
                for ins in rsqrt(rstd, ssq, half, bits):
                    link(m, k, ins)
                    k += 1
                link(m, k, v.tensor_tensor(cen[:], cen[:], pairs(rstd[:]), ALU.mult))
                link(m, k + 1, v.tensor_tensor(cen[:], cen[:], g.unsqueeze(1).to_broadcast([P, PAIR, D]), ALU.mult))
                ins = v.tensor_tensor(last, cen[:], b.unsqueeze(1).to_broadcast([P, PAIR, D]), ALU.add)
                if ready is None:
                    link(m, k + 2, ins)
                else:
                    ins.then_inc(ready, 1)

            def divide_sums(m):
                dve.wait_ge(nsum_loaded, 16 * (m + 1))
                link(m, 0, v.tensor_scalar(zrec[:], nsum[:, :, D:SW], 1e-6, None, ALU.add))
                link(m, 1, v.reciprocal(zrec[:], zrec[:]))
                v.tensor_tensor(attn[:].rearrange("p w (h d) -> p w h d", h=H),
                                nsum[:, :, 0:D].rearrange("p w (h d) -> p w h d", h=H),
                                zrec[:].unsqueeze(3).to_broadcast([P, PAIR, H, DH]), ALU.mult).then_inc(attn_ready, 1)

            def first_norm(l, j, m):
                dve.wait_ge(attn_projected, done(m))
                link(m, 2, v.tensor_tensor(res[:], no_bank[:, 0:PAIR * D].rearrange("p (w d) -> p w d", w=PAIR),
                                           h_all[:, bass.ds(j * PAIR, PAIR), :], ALU.add))
                norm(m, 3, res[:], norm_sb[:, l, 0, :], norm_sb[:, l, 1, :], h1[:], h1_ready)

            def second_norm(l, j, m):
                dve.wait_ge(ffn_ready, done(m))
                dve.wait_ge(h1_ready, done(m))
                link(m, 3 + NORM_STEPS, v.tensor_tensor(res[:], no_bank[:, 0:PAIR * D].rearrange("p (w d) -> p w d", w=PAIR),
                                            h1[:], ALU.add))
                if l + 1 < L:
                    norm(m, 4 + NORM_STEPS, res[:], norm_sb[:, l, 2, :], norm_sb[:, l, 3, :], h2[:], h2_ready)
                    dve.wait_ge(h2_ready, done(m + ITERS))
                    link(m, NODE_STEPS - 1, v.tensor_scalar(h_all[:, bass.ds(j * PAIR, PAIR), :], h2[:], 1.0, None, ALU.mult))
                else:
                    norm(m, 4 + NORM_STEPS, res[:], norm_sb[:, l, 2, :], norm_sb[:, l, 3, :], sq[:], None)
                    xw = x_all[:, bass.ds(j * PAIR, PAIR), :]
                    v.tensor_tensor(xw, sq[:], xw, ALU.add).then_inc(h2_ready, 1)

            def split_q(b, first=False):
                def step(k, ins):
                    ins.then_inc(split_step, 1)
                    dve.wait_ge(split_step, b * SPLIT_STEPS + (k + CREDIT + 1))
                dve.wait_ge(kvq_staged, done(b))
                if not first:
                    dve.wait_ge(q_stored, 16 * b)
                q = kvq[:, :, 2 * D:3 * D]
                step(0, v.tensor_copy(q_split[:, :, 0:D], q))
                step(1, v.tensor_tensor(q_rest[:], q, q_split[:, :, 0:D], ALU.subtract))
                step(2, v.tensor_copy(q_split[:, :, D:2 * D], q_rest[:]))
                v.tensor_tensor(q_split[:, :, 2 * D:3 * D], q_rest[:], q_split[:, :, D:2 * D], ALU.subtract)\
                    .then_inc(q_split_ready, 1)

            def stage_src(g, s):
                v.tensor_copy(src_slot[:, s % RING, :], src_all[:, bass.ds(g * TILES, TILES)]).then_inc(src_staged, 1)

            def build_onehot(g, s):
                v.tensor_tensor(onehot[:, s % 2], iota_ps.unsqueeze(1).to_broadcast([P, TILES + 1, P]),
                                rel[:, bass.ds(g, 1), :].rearrange("p a t -> p (a t)").unsqueeze(2)
                                .to_broadcast([P, TILES + 1, P]), ALU.is_equal).then_inc(onehot_built, 1)

            def edge_scores(l, i, s, n):
                dve.wait_ge(kv_gathered[s], 16 * TILES * (l * ITERS + i + 1))
                dve.wait_ge(edge_projected, done(n))
                v.tensor_tensor(prod[:], kv[:, s, :, 0:D], e_bank[:], ALU.mult).then_inc(key_used, 1)
                dve.wait_ge(query_spread, done(n))
                dve.wait_ge(key_used, done(n))
                v.tensor_tensor(prod[:], prod[:], q_bank[:], ALU.mult).then_inc(query_used, 1)
                dve.wait_ge(query_used, done(n))
                v.tensor_reduce(logit[:], prod[:].rearrange("p t (h d) -> p (t h) d", h=H), X, ALU.add)\
                    .then_inc(logit_ready, 1)
                dve.wait_ge(logit_ready, done(n))
                v.tensor_scalar(clip[:], logit[:], -5.0 * DH ** 0.5, 5.0 * DH ** 0.5, ALU.max, ALU.min)\
                    .then_inc(clip_ready, 1)

            def messages(s, n):
                dve.wait_ge(score_ready, done(n))
                v.tensor_tensor(msg[:, s % 2, 0:TILES, 0:D].rearrange("p t (h d) -> p t h d", h=H),
                                kv[:, s, :, D:2 * D].rearrange("p t (h d) -> p t h d", h=H),
                                msg[:, s % 2, 0:TILES, D:SW].unsqueeze(3).to_broadcast([P, TILES, H, DH]),
                                ALU.mult).then_inc(msg_ready, 1)

            def take_h0(j):
                v.tensor_copy(h2[:], h_all[:, bass.ds(j * PAIR, PAIR), :]).then_inc(h2_ready, 1)

            take_h0(0)
            split_q(0, first=True)
            with dve.Fori(1, ITERS) as j:
                take_h0(j)
                split_q(j)

            dve.wait_ge(bad_summed, 1)
            v.tensor_copy(flag[:], nt_bank[0:1, 0:1]).then_inc(flag_ready, 1)
            dve.wait_ge(flag_ready, 1)
            bad = dve.value_load(flag[0:1, 0:1], min_val=0, max_val=P)
            with dve.If(bad < 1):
                for s in range(IDX_AHEAD):
                    v.tensor_copy(src_slot[:, s, :], src_all[:, s * TILES:(s + 1) * TILES]).then_inc(src_staged, 1)
                build_onehot(0, 0)
                for l in range(L):
                    def one_pass(i, edges, nodes):
                        m = l * ITERS + i - LAG
                        for s in range(RING):
                            n = l * GROUPS + 4 * i + s
                            if edges:
                                stage_src(4 * i + s + IDX_AHEAD, s + IDX_AHEAD)
                                build_onehot(4 * i + s + 1, s + 1)
                                edge_scores(l, i, s, n)
                                messages(s, n)
                            if nodes and s == 0:
                                divide_sums(m)
                            if nodes and s == 1:
                                first_norm(l, i - LAG, m)
                            if nodes and s == 3:
                                second_norm(l, i - LAG, m)
                                if l + 1 < L:
                                    split_q(m + ITERS)
                    with dve.Fori(0, LAG) as i:
                        one_pass(i, True, False)
                    with dve.Fori(LAG, ITERS) as i:
                        one_pass(i, True, True)
                    with dve.Fori(ITERS, ITERS + LAG) as i:
                        one_pass(i, False, True)
            with dve.Else():
                for l in range(L):
                    with dve.Fori(0, EDGE_TILES) as t:
                        n = l * EDGE_TILES + t

                        def step(k, ins):
                            ins.then_inc(g_step, 1)
                            dve.wait_ge(g_step, n * G_STEPS + (k + 1))

                        step(0, v.tensor_copy(g_src[:], src_all[:, bass.ds(t, 1)]))
                        step(1, v.tensor_copy(g_dst[:], dst_all[:, bass.ds(t, 1)]))
                        step(2, v.tensor_copy(g_dstf[:], dst_f[:, bass.ds(t, 1)]))
                        v.tensor_copy(g_bc[:], g_dstf[:].to_broadcast([P, P])).then_inc(g_indexed, 1)
                        dve.wait_ge(g_projected, n + 1)
                        step(3, v.tensor_scalar(g_same[:], acc_bank[:, 0:P], g_dstf[:, 0:1], None, ALU.is_equal))
                        step(4, v.tensor_tensor(g_tmp[:], g_same[:], below[:], ALU.mult))
                        step(5, v.tensor_reduce(g_dup[:, 0:1], g_tmp[:], X, ALU.max))
                        step(6, v.tensor_tensor(g_dup[:, 1:2], dump_f[:], g_dstf[:], ALU.subtract))
                        step(7, v.tensor_tensor(g_dup[:, 1:2], g_dup[:, 1:2], g_dup[:, 0:1], ALU.mult))
                        step(8, v.tensor_tensor(g_to[:], g_dup[:, 1:2], g_dstf[:], ALU.add))
                        dve.wait_ge(g_gathered, 32 * (n + 1))
                        step(9, v.tensor_tensor(g_q[:], g_q3[:, 0:D], g_q3[:, D:2 * D], ALU.add))
                        step(10, v.tensor_tensor(g_q[:], g_q[:], g_q3[:, 2 * D:3 * D], ALU.add))
                        v.tensor_tensor(prod[:, 0, :], g_kv[:, 0:D], e_bank[:, 0, :], ALU.mult).then_inc(key_used, 1)
                        dve.wait_ge(key_used, done(n))
                        v.tensor_tensor(prod[:, 0, :], prod[:, 0, :], g_q[:], ALU.mult).then_inc(query_used, 1)
                        dve.wait_ge(query_used, done(n))
                        v.tensor_reduce(logit[:, 0:H], prod[:, 0, :].rearrange("p (h d) -> p h d", h=H), X, ALU.add)\
                            .then_inc(logit_ready, 1)
                        dve.wait_ge(logit_ready, done(n))
                        v.tensor_scalar(clip[:, 0:H], logit[:, 0:H], -5.0 * DH ** 0.5, 5.0 * DH ** 0.5, ALU.max, ALU.min)\
                            .then_inc(g_clipped, 1)
                        dve.wait_ge(g_scored, n + 1)
                        v.tensor_tensor(g_msg[:, 0:D].rearrange("p (h d) -> p h d", h=H),
                                        g_kv[:, D:2 * D].rearrange("p (h d) -> p h d", h=H),
                                        g_msg[:, D:SW].unsqueeze(2).to_broadcast([P, H, DH]), ALU.mult)\
                            .then_inc(g_msg_ready, 1)
                        dve.wait_ge(g_summed, n + 1)
                        v.tensor_copy(g_sum[:], q_bank[:].rearrange("p t d -> p (t d)")[:, 0:SW]).then_inc(g_sum_ready, 1)
                        dve.wait_ge(g_added, 16 * (n + 1))
                    with dve.Fori(0, ITERS) as j:
                        m = l * ITERS + j
                        divide_sums(m)
                        first_norm(l, j, m)
                        second_norm(l, j, m)
                        if l + 1 < L:
                            split_q(m + ITERS)


_WEIGHTS = ("WE", "WO", "bO", "ln1_g", "ln1_b", "W1", "b1", "W2", "b2", "ln2_g", "ln2_b")


def kernel(**inputs):
    import concourse.bacc as _bacc
    from concourse.bass_utils import run_bass_kernel_spmd as _run

    def get(name):
        return np.asarray(inputs[name])

    x = np.zeros((NP_, D), np.float32)
    x[:N] = get("x")
    x = x.reshape(WINDOWS, P, D).transpose(1, 0, 2)
    src = np.zeros(EP, np.int32)
    src[:E] = get("src")
    src = src.reshape(EDGE_TILES, P).T
    src = np.concatenate([src, src[:, :IDX_AHEAD * TILES]], axis=1)
    dst = np.full(EP, NP_ - 1, np.int32)
    dst[:E] = get("dst")
    base = dst[::GE]
    dst = dst.reshape(EDGE_TILES, P).T
    attr = np.zeros((D, EP), np.float32)
    attr[:, :E] = get("edge_attr_64").T
    wkvq = np.concatenate([get("L0_gnn_WK"), get("L0_gnn_WV"), get("L0_gnn_WQ")], axis=2)
    w = {k: get("L0_gnn_" + k) for k in _WEIGHTS}
    w["b1"] = w["b1"].T
    arrays = dict(x=x, src=src, dst=dst, base=base, edge_attr_t=attr, wkvq=wkvq, we=w["WE"], wo=w["WO"], bo=w["bO"],
                  g1=w["ln1_g"], be1=w["ln1_b"], w1=w["W1"], b1=w["b1"], w2=w["W2"], b2=w["b2"], g2=w["ln2_g"],
                  be2=w["ln2_b"])

    nc = _bacc.Bacc("TRN2", target_bir_lowering=False, num_devices=1)
    maps, aps = {}, {}
    for name, a in arrays.items():
        a = np.ascontiguousarray(a)
        maps[f"in_{name}"] = a
        aps[name] = nc.dram_tensor(f"in_{name}", a.shape, mybir.dt.from_np(a.dtype), kind="ExternalInput").ap()
    aps["out"] = nc.dram_tensor("out_nodes", (P, WINDOWS, D), F32, kind="ExternalOutput").ap()
    gnn(nc, **aps)
    r = _run(nc, [maps], core_ids=[0])
    got = np.asarray(r.results[0]["out_nodes"])
    return got.transpose(1, 0, 2).reshape(NP_, D)[:N]
```

```python
from contextlib import ExitStack

import numpy as np
import concourse.bass as bass
from concourse import mybir

F32 = mybir.dt.float32
BF16 = mybir.dt.bfloat16
I32 = mybir.dt.int32
ALU = mybir.AluOpType
ACT = mybir.ActivationFunctionType
X = mybir.AxisListType.X

P = 128
N, E, D, H, L = 12500, 200000, 64, 4, 2
DH = D // H
HID = 2 * D
EPS = 1e-5
TILES = 8
RING = 4
PAIR = 2
GE = TILES * P
ITERS = -(-E // (RING * GE))
GROUPS = ITERS * RING
EDGE_TILES = GROUPS * TILES
EP = GROUPS * GE
WINDOWS = PAIR * ITERS
NP_ = WINDOWS * P
assert NP_ >= N and GROUPS % 2 == 0
LAG = 2
WIN = 80
Q_ROWS = NP_ + P
DUMP = NP_ + P
S_ROWS = NP_ + 2 * P
SW = D + H
CREDIT = 4
NEWTON = 3
RSQRT_MAGIC = float(0x5F3759DF)
IDX_AHEAD = 3


def done(n):
    return n + (CREDIT + 1)


def gnn(nc, x, src, dst, base, edge_attr_t, wkvq, we, wo, bo, g1, be1, w1, b1, w2, b2, g2, be2, out):
    ctx = ExitStack()
    with ctx:
        def sb(name, shape, dt=F32):
            return ctx.enter_context(nc.sbuf_tensor(name, shape, dt))

        def bank(name, shape, dt=F32):
            return ctx.enter_context(nc.psum_tensor(name, shape, dt))

        def sem(name):
            return ctx.enter_context(nc.semaphore(name))

        kv_table = [nc.dram_tensor(f"kv_table{l}", (NP_, 2 * D), F32).ap() for l in range(L)]
        q_table = [nc.dram_tensor(f"q_table{l}", (Q_ROWS, 3 * D), BF16).ap() for l in range(L)]
        sums = [nc.dram_tensor(f"sums{l}", (S_ROWS, SW), F32).ap() for l in range(L)]

        x_all = sb("x_all", [P, WINDOWS, D])
        h_all = sb("h_all", [P, WINDOWS, D])
        src_all = sb("src_all", [P, (GROUPS + IDX_AHEAD) * TILES], I32)
        dst_all = sb("dst_all", [P, EDGE_TILES], I32)
        base_all = sb("base_all", [P, GROUPS], I32)
        rel = sb("rel", [P, GROUPS + 2, TILES])
        carry_rel = sb("carry_rel", [P, GROUPS + 1])
        src_slot = sb("src_slot", [P, RING, TILES], I32)
        kv = sb("kv", [P, RING, TILES, 2 * D])
        attr = sb("attr", [2 * D, RING, GE // 2])
        q_win = sb("q_win", [WIN, 2, 3 * D], BF16)
        onehot = sb("onehot", [P, RING, TILES, WIN], BF16)
        onehot_t = sb("onehot_t", [WIN, 2, TILES, P], BF16)
        carry_onehot = sb("carry_onehot", [WIN, RING, WIN])
        prod = sb("prod", [P, TILES, D])
        logit = sb("logit", [P, TILES * H])
        clip = sb("clip", [P, TILES * H])
        msg = sb("msg", [P, TILES, SW])
        msg_rest = sb("msg_rest", [P, TILES, SW])
        msg3 = sb("msg3", [P, 2, 3, TILES, SW], BF16)
        carry = sb("carry", [WIN, 2, SW])
        nsum = sb("nsum", [P, PAIR, SW])
        zrec = sb("zrec", [P, PAIR, H])
        attn = sb("attn", [P, PAIR, D])
        attn_t = sb("attn_t", [D + 1, PAIR * P])
        res = sb("res", [P, PAIR, D])
        cen = sb("cen", [P, PAIR, D])
        sq = sb("sq", [P, PAIR, D])
        tot = sb("tot", [P, PAIR])
        ssq = sb("ssq", [P, PAIR])
        rstd = sb("rstd", [P, PAIR])
        half = sb("half", [P, PAIR])
        bits = sb("bits", [P, PAIR], I32)
        h1 = sb("h1", [P, PAIR, D])
        h1_t = sb("h1_t", [D, PAIR * P])
        hid = sb("hid", [HID, PAIR * P])
        h2 = sb("h2", [P, PAIR, D])
        h2_t = sb("h2_t", [D, PAIR * P])
        kvq = sb("kvq", [P, PAIR, 3 * D])
        q_rest = sb("q_rest", [P, PAIR, D])
        q_split = sb("q_split", [P, PAIR, 3 * D], BF16)
        CH = 14
        assert WINDOWS % CH == 0
        c_cen = sb("c_cen", [P, CH, D])
        c_sq = sb("c_sq", [P, CH, D])
        c_tot = sb("c_tot", [P, CH])
        c_ssq = sb("c_ssq", [P, CH])
        c_rstd = sb("c_rstd", [P, CH])
        c_half = sb("c_half", [P, CH])
        c_bits = sb("c_bits", [P, CH], I32)
        wkvq_sb = sb("wkvq_sb", [D, L, 3 * D])
        we_sb = sb("we_sb", [2 * D, L, 2 * D])
        wo_sb = sb("wo_sb", [D + 1, L, D])
        w1_sb = sb("w1_sb", [D, L, HID])
        b1_sb = sb("b1_sb", [HID, L])
        w2_sb = sb("w2_sb", [HID, L, D])
        b2_sb = sb("b2_sb", [1, L, D])
        norm_sb = sb("norm_sb", [P, L, 4, D])
        ones = sb("ones", [P, P])
        ident = sb("ident", [P, P])
        ident_b = sb("ident_b", [P, P], BF16)
        iota_i = sb("iota_i", [P, P], I32)
        part_i = sb("part_i", [P, 1], I32)
        iota_f = sb("iota_f", [P, P])
        part_f = sb("part_f", [P, 1])
        dump_f = sb("dump_f", [P, 1])
        below = sb("below", [P, P])
        zeros = sb("zeros", [P, S_ROWS // P * SW // 4])
        chk = sb("chk", [P, 8])
        step_f = sb("step_f", [P, GROUPS])
        base_f = sb("base_f", [P, GROUPS])
        limit_i = sb("limit_i", [P, ITERS - LAG], I32)
        limit_f = sb("limit_f", [P, ITERS - LAG])
        dst_f = sb("dst_f", [P, EDGE_TILES])
        flag = sb("flag", [1, 1], I32)
        g_src = sb("g_src", [P, 1], I32)
        g_dst = sb("g_dst", [P, 1], I32)
        g_to = sb("g_to", [P, 1], I32)
        g_dstf = sb("g_dstf", [P, 1])
        g_kv = sb("g_kv", [P, 2 * D])
        g_q3 = sb("g_q3", [P, 3 * D], BF16)
        g_q = sb("g_q", [P, D])
        g_attr = sb("g_attr", [D, P])
        g_dup = sb("g_dup", [P, 4])
        g_bc = sb("g_bc", [P, P])
        g_same = sb("g_same", [P, P])
        g_tmp = sb("g_tmp", [P, P])
        g_msg = sb("g_msg", [P, SW])
        g_sum = sb("g_sum", [P, SW])

        e_bank = bank("e_bank", [P, TILES, D])
        q_bank = bank("q_bank", [P, TILES, D])
        t_bank = bank("t_bank", [WIN, TILES, P], BF16)
        acc_bank = bank("acc_bank", [P, 512])
        nt_bank = bank("nt_bank", [P, 512])
        hid_bank = bank("hid_bank", [P, 512])
        no_bank = bank("no_bank", [P, 512])
        iota_bank = bank("iota_bank", [P, 512])
        acc = acc_bank[0:WIN, 0:SW]
        iota_ps = iota_bank[:, 0:WIN]
        ffn = hid_bank[:, PAIR * P:PAIR * P + PAIR * D]

        weights_loaded = sem("weights_loaded")
        wo_loaded = sem("wo_loaded")
        x_loaded = sem("x_loaded")
        indices_loaded = sem("indices_loaded")
        attr_loaded = [sem(f"attr_loaded{s}") for s in range(RING)]
        q_win_loaded = [sem(f"q_win_loaded{s}") for s in range(2)]
        kv_gathered = [sem(f"kv_gathered{s}") for s in range(RING)]
        q_pad_zeroed = sem("q_pad_zeroed")
        sums_written = sem("sums_written")
        nsum_loaded = sem("nsum_loaded")
        kv_stored = sem("kv_stored")
        q_stored = sem("q_stored")
        out_stored = sem("out_stored")
        pool_consts = sem("pool_consts")
        dve_consts = sem("dve_consts")
        h0_ready = sem("h0_ready")
        h0_step = sem("h0_step")
        chk_step = sem("chk_step")
        bad_ready = sem("bad_ready")
        bad_summed = sem("bad_summed")
        flag_ready = sem("flag_ready")
        src_staged = sem("src_staged")
        onehot_built = sem("onehot_built")
        carry_onehot_built = sem("carry_onehot_built")
        onehot_turned = sem("onehot_turned")
        onehot_t_ready = sem("onehot_t_ready")
        edge_projected = sem("edge_projected")
        query_spread = sem("query_spread")
        key_used = sem("key_used")
        query_used = sem("query_used")
        logit_ready = sem("logit_ready")
        clip_ready = sem("clip_ready")
        score_ready = sem("score_ready")
        msg_ready = sem("msg_ready")
        msg_hi_ready = sem("msg_hi_ready")
        msg_rest_ready = sem("msg_rest_ready")
        msg_mid_ready = sem("msg_mid_ready")
        msg_lo_ready = sem("msg_lo_ready")
        group_summed = sem("group_summed")
        carry_ready = sem("carry_ready")
        attn_ready = sem("attn_ready")
        attn_turned = sem("attn_turned")
        attn_t_ready = sem("attn_t_ready")
        attn_projected = sem("attn_projected")
        attn_used = sem("attn_used")
        h1_ready = sem("h1_ready")
        h1_turned = sem("h1_turned")
        h1_t_ready = sem("h1_t_ready")
        hid_ready = sem("hid_ready")
        relu_ready = sem("relu_ready")
        ffn_ready = sem("ffn_ready")
        h2_ready = sem("h2_ready")
        h2_turned = sem("h2_turned")
        h2_t_ready = sem("h2_t_ready")
        kvq_projected = sem("kvq_projected")
        kvq_staged = sem("kvq_staged")
        q_split_ready = sem("q_split_ready")
        divide_step = sem("divide_step")
        norm1_step = sem("norm1_step")
        norm2_step = sem("norm2_step")
        split_step = sem("split_step")
        sp_passed = sem("sp_passed")
        pool_passed = sem("pool_passed")
        pe_passed = sem("pe_passed")
        g_indexed = sem("g_indexed")
        g_attr_loaded = sem("g_attr_loaded")
        g_gathered = [sem(f"g_gathered{l}") for l in range(L)]
        g_step = sem("g_step")
        g_projected = sem("g_projected")
        g_clipped = sem("g_clipped")
        g_scored = sem("g_scored")
        g_msg_ready = sem("g_msg_ready")
        g_summed = sem("g_summed")
        g_sum_ready = sem("g_sum_ready")
        g_added = [sem(f"g_added{l}") for l in range(L)]

        ZERO_FILLS = 4 * L
        DIVIDE_STEPS = 2
        RSQRT_STEPS = 4 + 3 * NEWTON
        NORM_STEPS = 1 + 4 + RSQRT_STEPS + 3 + 1
        SPLIT_STEPS = 3
        G_STEPS = 11
        block = ctx.enter_context(nc.Block())

        def window_rows(table, j):
            return table[bass.ds(j * (PAIR * P), PAIR * P), :].rearrange("(w p) c -> p w c", p=P)

        @block.sync
        def _(sp):
            sp.dma_start(x_all[:], x).then_inc(x_loaded, 16)
            sp.dma_start(src_all[:], src).then_inc(indices_loaded, 16)
            sp.dma_start(dst_all[:], dst).then_inc(indices_loaded, 16)
            sp.dma_start(base_all[:], base.partition_broadcast(P)).then_inc(indices_loaded, 16)
            sp.dma_start(wkvq_sb[:], wkvq.rearrange("l k n -> k l n")).then_inc(weights_loaded, 16)
            sp.wait_ge(pool_consts, 1)
            for half in range(2):
                on = slice(half * D, (half + 1) * D)
                sp.dma_start(we_sb[on, :, on], we.rearrange("l k n -> k l n")).then_inc(weights_loaded, 16)
            sp.dma_start(wo_sb[0:D], wo.rearrange("l k n -> k l n")).then_inc(weights_loaded, 16)
            sp.dma_start(wo_sb[D:D + 1], bo.unsqueeze(0)).then_inc(weights_loaded, 16)
            sp.dma_start(w1_sb[:], w1.rearrange("l k n -> k l n")).then_inc(weights_loaded, 16)
            sp.dma_start(b1_sb[:], b1).then_inc(weights_loaded, 16)
            sp.dma_start(w2_sb[:], w2.rearrange("l k n -> k l n")).then_inc(weights_loaded, 16)
            sp.dma_start(b2_sb[:], b2.unsqueeze(0)).then_inc(weights_loaded, 16)
            for k, a in enumerate((g1, be1, g2, be2)):
                sp.dma_start(norm_sb[:, :, k, :], a.partition_broadcast(P)).then_inc(weights_loaded, 16)
            sp.wait_ge(pool_consts, 2)
            part = S_ROWS // 4
            for l in range(L):
                for k in range(4):
                    sp.dma_start(sums[l][k * part:(k + 1) * part, :].rearrange("(p r) c -> p (r c)", p=P),
                                 zeros[:]).then_inc(sums_written, 16)
                sp.dma_start(q_table[l][NP_:Q_ROWS, :], zeros[:, 0:3 * D // 2].bitcast(BF16)).then_inc(q_pad_zeroed, 16)
            sp.wait_ge(q_pad_zeroed, 16 * L)
            sp.wait_ge(indices_loaded, 48)

            def attr_group(g):
                return edge_attr_t[bass.ds(g, 1)].rearrange("a h f e -> (a h f) e")

            def load_group(l, i, s):
                n = l * GROUPS + 4 * i + s
                sp.wait_ge(edge_projected, done(n - RING))
                sp.dma_start(attr[:, s, :], attr_group(4 * i + s)).then_inc(attr_loaded[s], 16)
                first = sp.value_load(base_all[0:1, bass.ds(4 * i + s, 1)], min_val=0, max_val=NP_ - 1)
                sp.wait_ge(query_spread, done(n - 2))
                sp.dma_start(q_win[:, s % 2, :], q_table[l][bass.ds(first, WIN), :]).then_inc(q_win_loaded[s % 2], 16)

            def load_nsum(l, j, written):
                sp.wait_ge(sums_written, written)
                sp.sem_inc(sp_passed, 1)
                sp.wait_ge(attn_ready, done(l * ITERS + j - 1))
                sp.dma_start(nsum[:], window_rows(sums[l], j)).then_inc(nsum_loaded, 16)

            sp.wait_ge(flag_ready, 1)
            bad = sp.value_load(flag[0:1, 0:1], min_val=0, max_val=P)
            with sp.If(bad < 1):
                for l in range(L):
                    sp.wait_ge(q_stored, 16 * ITERS * (l + 1))
                    for i in range(LAG):
                        for s in range(RING):
                            load_group(l, i, s)
                    with sp.Fori(LAG, ITERS) as i:
                        for s in range(RING):
                            load_group(l, i, s)
                            if s == 0:
                                load_nsum(l, i - LAG, 16 * (ZERO_FILLS + l * GROUPS) + 16 * (4 * i - 2))
                    for i in range(ITERS, ITERS + LAG):
                        load_nsum(l, i - LAG, 16 * (ZERO_FILLS + (l + 1) * GROUPS))
            with sp.Else():
                for l in range(L):
                    with sp.Fori(0, EDGE_TILES // 4) as q:
                        for t in range(4):
                            sp.dma_start(g_attr[:], edge_attr_t.rearrange("g h f e -> (g h) f e")[
                                bass.ds(q, 1), :, t * P:(t + 1) * P].rearrange("a f e -> (a f) e"))\
                                .then_inc(g_attr_loaded, 16)
                            sp.wait_ge(g_projected, l * EDGE_TILES + 4 * q + (t + 1))
                            sp.sem_inc(sp_passed, 1)
                    sp.wait_ge(g_added[l], 16 * EDGE_TILES)
                    with sp.Fori(0, ITERS) as j:
                        load_nsum(l, j, 16 * ZERO_FILLS)

        @block.gpsimd
        def _(pool):
            nc.gpsimd.memset(we_sb[:], 0.0).then_inc(pool_consts, 1)
            nc.gpsimd.memset(zeros[:], 0.0).then_inc(pool_consts, 1)
            nc.gpsimd.memset(ones[:], 1.0).then_inc(pool_consts, 1)
            nc.gpsimd.memset(carry[:], 0.0).then_inc(pool_consts, 1)
            nc.gpsimd.memset(attn_t[:], 1.0).then_inc(pool_consts, 1)
            nc.gpsimd.iota(iota_i[:], [[1, P]], base=0, channel_multiplier=0).then_inc(pool_consts, 1)
            nc.gpsimd.iota(part_i[:], [[0, 1]], base=0, channel_multiplier=1).then_inc(pool_consts, 1)
            nc.gpsimd.iota(limit_i[:], [[PAIR * P, ITERS - LAG]], base=PAIR * P, channel_multiplier=0)\
                .then_inc(pool_consts, 1)

            pool.wait_ge(flag_ready, 1)
            bad = pool.value_load(flag[0:1, 0:1], min_val=0, max_val=P)
            with pool.If(bad < 1):
                for l in range(L):
                    pool.wait_ge(kv_stored, 16 * ITERS * (l + 1))
                    with pool.Fori(0, ITERS) as i:
                        for s in range(RING):
                            n = l * GROUPS + 4 * i + s
                            pool.wait_ge(src_staged, done(n))
                            pool.wait_ge(msg_ready, done(n - RING))
                            pool.sem_inc(pool_passed, 1)
                            for t in range(TILES):
                                nc.gpsimd.indirect_dma_start(
                                    out=kv[:, s, t, :], out_offset=None, in_=kv_table[l][:, :],
                                    in_offset=bass.IndirectOffsetOnAxis(ap=src_slot[:, s, t:t + 1], axis=0),
                                ).then_inc(kv_gathered[s], 16)
            with pool.Else():
                for l in range(L):
                    pool.wait_ge(q_stored, 16 * ITERS * (l + 1))
                    pool.wait_ge(kv_stored, 16 * ITERS * (l + 1))
                    pool.wait_ge(q_pad_zeroed, 16 * L)
                    pool.wait_ge(sums_written, 16 * ZERO_FILLS)
                    with pool.Fori(0, EDGE_TILES) as t:
                        n = l * EDGE_TILES + t
                        pool.wait_ge(g_indexed, n + 1)
                        pool.sem_inc(pool_passed, 1)
                        nc.gpsimd.indirect_dma_start(
                            out=g_kv[:], out_offset=None, in_=kv_table[l][:, :],
                            in_offset=bass.IndirectOffsetOnAxis(ap=g_src[:, 0:1], axis=0)).then_inc(g_gathered[l], 16)
                        nc.gpsimd.indirect_dma_start(
                            out=g_q3[:], out_offset=None, in_=q_table[l][:, :],
                            in_offset=bass.IndirectOffsetOnAxis(ap=g_dst[:, 0:1], axis=0)).then_inc(g_gathered[l], 16)
                        pool.wait_ge(g_sum_ready, n + 1)
                        pool.sem_inc(pool_passed, 1)
                        nc.gpsimd.indirect_dma_start(
                            out=sums[l][:, :], out_offset=bass.IndirectOffsetOnAxis(ap=g_to[:, 0:1], axis=0),
                            in_=g_sum[:], in_offset=None, compute_op=ALU.add).then_inc(g_added[l], 16)
                        pool.wait_ge(g_added[l], 16 * (t + 1))
                        pool.sem_inc(pool_passed, 1)

        @block.tensor
        def _(pe):
            for done_by_pe in (onehot_turned, edge_projected, query_spread, group_summed, attn_turned,
                               attn_projected, h1_turned, hid_ready, ffn_ready, h2_turned, kvq_projected):
                pe.sem_inc(done_by_pe, CREDIT)

            def turn_attn(m):
                pe.wait_ge(attn_ready, done(m))
                pe.sem_inc(pe_passed, 1)
                for w in range(PAIR):
                    last = pe.transpose(nt_bank[0:D, w * P:(w + 1) * P], attn[:, w, :], ident[:])
                last.then_inc(attn_turned, 1)

            def project_attn(l, m, b):
                if l + 1 < L:
                    pe.wait_ge(kvq_staged, done(b + ITERS))
                pe.wait_ge(attn_t_ready, done(m))
                for w in range(PAIR):
                    last = pe.matmul(no_bank[:, w * D:(w + 1) * D], attn_t[:, w * P:(w + 1) * P], wo_sb[:, l, :],
                                     start=True, stop=True)
                last.then_inc(attn_projected, 1)

            def turn_h1(m):
                pe.wait_ge(h1_ready, done(m))
                pe.sem_inc(pe_passed, 1)
                for w in range(PAIR):
                    last = pe.transpose(nt_bank[0:D, w * P:(w + 1) * P], h1[:, w, :], ident[:])
                last.then_inc(h1_turned, 1)

            def project_hidden(l, m):
                pe.wait_ge(h1_t_ready, done(m))
                pe.matmul(hid_bank[:, 0:PAIR * P], w1_sb[:, l, :], h1_t[:], start=True, stop=True).then_inc(hid_ready, 1)

            def project_ffn(l, m):
                pe.wait_ge(relu_ready, done(m))
                for w in range(PAIR):
                    o = ffn[:, w * D:(w + 1) * D]
                    pe.matmul(o, hid[:, w * P:(w + 1) * P], w2_sb[:, l, :], start=True, stop=False)
                    last = pe.matmul(o, ones[0:1, :], b2_sb[:, l, :], start=False, stop=True)
                last.then_inc(ffn_ready, 1)

            def turn_h2(b):
                pe.wait_ge(h2_ready, done(b))
                pe.sem_inc(pe_passed, 1)
                for w in range(PAIR):
                    last = pe.transpose(nt_bank[0:D, w * P:(w + 1) * P], h2[:, w, :], ident[:])
                last.then_inc(h2_turned, 1)

            def project_kvq(l, b, a=None):
                pe.wait_ge(h2_t_ready, done(b))
                if a is not None:
                    pe.wait_ge(attn_used, done(a))
                pe.wait_ge(kvq_staged, done(b - 1))
                for w in range(PAIR):
                    last = pe.matmul(no_bank[:, w * 3 * D:(w + 1) * 3 * D], h2_t[:, w * P:(w + 1) * P],
                                     wkvq_sb[:, l, :], start=True, stop=True)
                last.then_inc(kvq_projected, 1)

            def turn_onehot(s, n):
                pe.wait_ge(onehot_built, done(n))
                pe.wait_ge(onehot_t_ready, done(n - 1))
                for t in range(TILES):
                    last = pe.transpose(t_bank[:, t, :], onehot[:, s % RING, t, :], ident_b[:])
                last.then_inc(onehot_turned, 1)

            def project_edges(l, i, s, n):
                pe.wait_ge(attr_loaded[s], 16 * (l * ITERS + i + 1))
                pe.wait_ge(key_used, done(n - 1))
                for t in range(TILES // 2):
                    last = pe.matmul(e_bank[:, t::TILES // 2, :], attr[:, s, t * P:(t + 1) * P], we_sb[:, l, :],
                                     start=True, stop=True)
                last.then_inc(edge_projected, 1)

            def spread_query(l, i, s, n):
                pe.wait_ge(onehot_t_ready, done(n))
                pe.wait_ge(q_win_loaded[s % 2], 16 * (2 * (l * ITERS + i) + s // 2 + 1))
                pe.wait_ge(query_used, done(n - 1))
                for t in range(TILES):
                    for k in range(3):
                        last = pe.matmul(q_bank[:, t, :], onehot_t[:, s % 2, t, :], q_win[:, s % 2, k * D:(k + 1) * D],
                                         start=(k == 0), stop=(k == 2))
                last.then_inc(query_spread, 1)

            def sum_group(s, n):
                pe.wait_ge(carry_onehot_built, done(n))
                pe.wait_ge(carry_ready, done(n - 1))
                pe.matmul(acc, carry_onehot[:, s % RING, :], carry[:, (s - 1) % 2, :], start=True, stop=False)
                pe.wait_ge(msg_lo_ready, done(n))
                for t in range(TILES):
                    for k in range(3):
                        last = pe.matmul(acc, onehot[:, s % RING, t, :], msg3[:, s % 2, k, t, :],
                                         start=False, stop=(t == TILES - 1 and k == 2))
                last.then_inc(group_summed, 1)

            pe.wait_ge(weights_loaded, 16 * 13)
            pe.wait_ge(dve_consts, 4)
            with pe.Fori(0, ITERS) as j:
                pe.wait_ge(h2_t_ready, done(j - 1))
                turn_h2(j)
                project_kvq(0, j)

            pe.wait_ge(bad_ready, 1)
            pe.matmul(nt_bank[0:1, 0:1], chk[:, 7:8], ones[:, 0:1], start=True, stop=True).then_inc(bad_summed, 1)
            pe.wait_ge(flag_ready, 1)
            bad = pe.value_load(flag[0:1, 0:1], min_val=0, max_val=P)
            with pe.If(bad < 1):
                turn_onehot(0, 0)
                for l in range(L):
                    def one_pass(i, edges=True, first_half=True, second_half=True, start=False):
                        m = l * ITERS + i - LAG
                        b = m - 1
                        for s in range(RING):
                            n = l * GROUPS + 4 * i + s
                            if edges:
                                project_edges(l, i, s, n)
                                spread_query(l, i, s, n)
                                turn_onehot(s + 1, n + 1)
                            if second_half and s == 0:
                                project_ffn(l, b)
                            if first_half and s == 1:
                                turn_attn(m)
                            if second_half and s == 2 and l + 1 < L:
                                turn_h2(b + ITERS)
                            if first_half and s == 3:
                                turn_h1(m)
                            if edges and not (start and s == 0):
                                sum_group(s - 1, n - 1)
                            if first_half and s == 1:
                                project_attn(l, m, m - 2)
                            if second_half and s == 2 and l + 1 < L:
                                project_kvq(l + 1, b + ITERS, m if first_half else None)
                            if first_half and s == 3:
                                project_hidden(l, m)

                    one_pass(0, first_half=False, second_half=False, start=True)
                    one_pass(1, first_half=False, second_half=False)
                    one_pass(2, second_half=False)
                    with pe.Fori(LAG + 1, ITERS) as i:
                        one_pass(i)
                    sum_group(RING - 1, (l + 1) * GROUPS - 1)
                    one_pass(ITERS, edges=False)
                    one_pass(ITERS + 1, edges=False)
                    one_pass(ITERS + 2, edges=False, first_half=False)
            with pe.Else():
                for l in range(L):
                    with pe.Fori(0, EDGE_TILES) as t:
                        n = l * EDGE_TILES + t
                        pe.wait_ge(g_attr_loaded, 16 * (n + 1))
                        pe.wait_ge(g_indexed, n + 1)
                        pe.matmul(e_bank[:, 0, :], g_attr[:], we_sb[0:D, l, 0:D], start=True, stop=True)
                        pe.transpose(acc_bank[:, 0:P], g_bc[:], ident[:]).then_inc(g_projected, 1)
                        pe.wait_ge(g_msg_ready, n + 1)
                        pe.matmul(q_bank[:].rearrange("p t d -> p (t d)")[:, 0:SW], g_same[:], g_msg[:],
                                  start=True, stop=True).then_inc(g_summed, 1)
                    with pe.Fori(0, ITERS) as j:
                        m = l * ITERS + j
                        turn_attn(m)
                        project_attn(l, m, m - 1)
                        turn_h1(m)
                        project_hidden(l, m)
                        project_ffn(l, m)
                        if l + 1 < L:
                            turn_h2(m + ITERS)
                            project_kvq(l + 1, m + ITERS, m)

        @block.scalar
        def _(act):
            for done_by_act in (onehot_t_ready, score_ready, msg_hi_ready, msg_mid_ready, carry_ready, attn_t_ready, h1_t_ready,
                                relu_ready, h2_t_ready, kvq_staged):
                act.sem_inc(done_by_act, CREDIT)

            def copy_attn_t(m):
                act.wait_ge(attn_turned, done(m))
                nc.scalar.copy(attn_t[0:D, :], nt_bank[0:D, 0:PAIR * P]).then_inc(attn_t_ready, 1)

            def copy_h1_t(m):
                act.wait_ge(h1_turned, done(m))
                nc.scalar.copy(h1_t[:], nt_bank[0:D, 0:PAIR * P]).then_inc(h1_t_ready, 1)

            def relu_hidden(l, m):
                act.wait_ge(hid_ready, done(m))
                nc.scalar.activation(hid[:], hid_bank[:, 0:PAIR * P], ACT.Relu, bias=b1_sb[:, l:l + 1])\
                    .then_inc(relu_ready, 1)

            def copy_h2_t(b):
                act.wait_ge(h2_turned, done(b))
                nc.scalar.copy(h2_t[:], nt_bank[0:D, 0:PAIR * P]).then_inc(h2_t_ready, 1)

            def store_kv(l, j, b, first=False):
                act.wait_ge(kvq_projected, done(b))
                act.wait_ge(q_split_ready, done(b - 1))
                if not first:
                    act.wait_ge(kv_stored, 16 * b)
                nc.scalar.copy(kvq[:].rearrange("p w c -> p (w c)"), no_bank[:, 0:PAIR * 3 * D]).then_inc(kvq_staged, 1)
                act.wait_ge(kvq_staged, done(b))
                act.dma_start(window_rows(kv_table[l], j), kvq[:, :, 0:2 * D]).then_inc(kv_stored, 16)

            def store_q(l, j, b):
                act.wait_ge(q_split_ready, done(b))
                act.dma_start(window_rows(q_table[l], j), q_split[:]).then_inc(q_stored, 16)

            def copy_onehot_t(s, n):
                act.wait_ge(onehot_turned, done(n))
                nc.scalar.copy(onehot_t[:, s % 2], t_bank[:]).then_inc(onehot_t_ready, 1)

            def exp_scores(s, n):
                act.wait_ge(clip_ready, done(n))
                nc.scalar.activation(msg[:, :, D:SW], clip[:].rearrange("p (t h) -> p t h", h=H), ACT.Exp,
                                     scale=DH ** -0.5).then_inc(score_ready, 1)

            def msg_hi(s, n):
                act.wait_ge(msg_ready, done(n))
                nc.scalar.copy(msg3[:, s % 2, 0], msg[:]).then_inc(msg_hi_ready, 1)

            def msg_mid(s, n):
                act.wait_ge(msg_rest_ready, done(n))
                nc.scalar.copy(msg3[:, s % 2, 1], msg_rest[:]).then_inc(msg_mid_ready, 1)

            def write_sums(l, g, s, n):
                act.wait_ge(group_summed, done(n))
                nc.scalar.copy(carry[:, s % 2, :], acc).then_inc(carry_ready, 1)
                first = act.value_load(base_all[0:1, bass.ds(g, 1)], min_val=0, max_val=NP_ - 1)
                act.wait_ge(sums_written, 16 * ZERO_FILLS + 16 * n)
                act.wait_ge(carry_ready, done(n))
                act.dma_start(sums[l][bass.ds(first, WIN), :], carry[:, s % 2, :]).then_inc(sums_written, 16)

            copy_h2_t(0)
            store_kv(0, 0, 0, first=True)
            store_q(0, 0, 0)
            with act.Fori(1, ITERS) as j:
                copy_h2_t(j)
                store_kv(0, j, j)
                store_q(0, j, j)

            act.wait_ge(flag_ready, 1)
            bad = act.value_load(flag[0:1, 0:1], min_val=0, max_val=P)
            with act.If(bad < 1):
                copy_onehot_t(0, 0)

                def store_out(j, m):
                    act.wait_ge(h2_ready, done(m + ITERS))
                    act.dma_start(out[:, bass.ds(j * PAIR, PAIR), :], x_all[:, bass.ds(j * PAIR, PAIR), :])\
                        .then_inc(out_stored, 16)

                for l in range(L):
                    def one_pass(i, edges=True, first_half=True, second_half=True, start=False):
                        m = l * ITERS + i - LAG
                        b = m - 1
                        for s in range(RING):
                            n = l * GROUPS + 4 * i + s
                            if edges:
                                copy_onehot_t(s + 1, n + 1)
                                exp_scores(s, n)
                            if first_half and s == 1:
                                copy_attn_t(m)
                            if second_half and s == 2 and l + 1 < L:
                                copy_h2_t(b + ITERS)
                            if first_half and s == 3:
                                copy_h1_t(m)
                            if edges:
                                msg_hi(s, n)
                                msg_mid(s, n)
                                if not (start and s == 0):
                                    write_sums(l, 4 * i + s - 1, s - 1, n - 1)
                            if second_half and s == 2:
                                if l + 1 < L:
                                    store_kv(l + 1, i - LAG - 1, b + ITERS)
                                else:
                                    store_out(i - LAG - 1, b)
                            if first_half and s == 3:
                                relu_hidden(l, m)
                            if second_half and s == 3 and l + 1 < L:
                                store_q(l + 1, i - LAG - 1, b + ITERS)

                    one_pass(0, first_half=False, second_half=False, start=True)
                    one_pass(1, first_half=False, second_half=False)
                    one_pass(2, second_half=False)
                    with act.Fori(LAG + 1, ITERS) as i:
                        one_pass(i)
                    write_sums(l, GROUPS - 1, RING - 1, (l + 1) * GROUPS - 1)
                    one_pass(ITERS, edges=False)
                    one_pass(ITERS + 1, edges=False)
                    one_pass(ITERS + 2, edges=False, first_half=False)
                act.wait_ge(sums_written, 16 * (ZERO_FILLS + L * GROUPS))
            with act.Else():
                for l in range(L):
                    with act.Fori(0, EDGE_TILES) as t:
                        n = l * EDGE_TILES + t
                        act.wait_ge(g_clipped, n + 1)
                        nc.scalar.activation(g_msg[:, D:SW], clip[:, 0:H], ACT.Exp, scale=DH ** -0.5).then_inc(g_scored, 1)
                    with act.Fori(0, ITERS) as j:
                        m = l * ITERS + j
                        copy_attn_t(m)
                        copy_h1_t(m)
                        relu_hidden(l, m)
                        if l + 1 < L:
                            copy_h2_t(m + ITERS)
                            store_kv(l + 1, j, m + ITERS)
                            store_q(l + 1, j, m + ITERS)
                        else:
                            act.wait_ge(h2_ready, done(m + ITERS))
                            act.dma_start(out[:, bass.ds(j * PAIR, PAIR), :], x_all[:, bass.ds(j * PAIR, PAIR), :])\
                                .then_inc(out_stored, 16)
            act.wait_ge(out_stored, 16 * ITERS)
            act.wait_ge(kv_stored, 16 * L * ITERS)
            act.wait_ge(q_stored, 16 * L * ITERS)

        @block.vector
        def _(dve):
            v = nc.vector
            for done_by_dve in (src_staged, onehot_built, carry_onehot_built, key_used, query_used, logit_ready,
                                clip_ready, msg_ready, msg_rest_ready, msg_lo_ready, attn_ready, attn_used, h1_ready,
                                h2_ready, q_split_ready, divide_step, norm1_step, norm2_step, split_step):
                dve.sem_inc(done_by_dve, CREDIT)

            def pairs(a):
                return a.unsqueeze(2).to_broadcast([P, PAIR, D])

            dve.wait_ge(pool_consts, 8)
            v.tensor_copy(iota_f[:], iota_i[:]).then_inc(chk_step, 1)
            v.tensor_copy(part_f[:], part_i[:]).then_inc(chk_step, 1)
            dve.wait_ge(chk_step, 2)
            v.tensor_copy(iota_ps, iota_f[:, 0:WIN]).then_inc(dve_consts, 1)
            v.tensor_scalar(ident[:], iota_f[:], part_f[:, 0:1], None, ALU.is_equal).then_inc(dve_consts, 1)
            v.tensor_scalar(ident_b[:], iota_f[:], part_f[:, 0:1], None, ALU.is_equal).then_inc(dve_consts, 1)
            v.tensor_scalar(below[:], iota_f[:], part_f[:, 0:1], None, ALU.is_lt).then_inc(dve_consts, 1)
            v.tensor_scalar(dump_f[:], part_f[:], float(DUMP), None, ALU.add).then_inc(chk_step, 1)

            def rsqrt_step(k, y, ssq, half, bits):
                if k == 0:
                    return v.tensor_scalar(ssq[:], ssq[:], 1.0 / D, EPS, ALU.mult, ALU.add)
                if k == 1:
                    return v.tensor_scalar(bits[:], ssq[:].bitcast(I32), 1, None, ALU.logical_shift_right)
                if k == 2:
                    return v.tensor_scalar(y[:].bitcast(I32), bits[:], -1.0, RSQRT_MAGIC, ALU.mult, ALU.add)
                if k == 3:
                    return v.tensor_scalar(half[:], ssq[:], -0.5, None, ALU.mult)
                if (k - 4) % 3 == 0:
                    return v.tensor_tensor(ssq[:], y[:], y[:], ALU.mult)
                if (k - 4) % 3 == 1:
                    return v.tensor_tensor(ssq[:], ssq[:], half[:], ALU.mult)
                return v.scalar_tensor_tensor(y[:], ssq[:], 1.5, y[:], ALU.add, ALU.mult)

            dve.wait_ge(x_loaded, 16)
            steps = [0]

            def h0_link(ins):
                steps[0] += 1
                ins.then_inc(h0_step, 1)
                dve.wait_ge(h0_step, steps[0])

            def chunk(a):
                return a.unsqueeze(2).to_broadcast([P, CH, D])

            for c in range(WINDOWS // CH):
                xc = x_all[:, c * CH:(c + 1) * CH, :]
                h0_link(v.tensor_reduce(c_tot[:], xc, X, ALU.add))
                h0_link(v.scalar_tensor_tensor(c_cen[:], chunk(c_tot[:]), -1.0 / D, xc, ALU.mult, ALU.add))
                h0_link(v.tensor_tensor(c_sq[:], c_cen[:], c_cen[:], ALU.mult))
                h0_link(v.tensor_reduce(c_ssq[:], c_sq[:], X, ALU.add))
                for k in range(RSQRT_STEPS):
                    h0_link(rsqrt_step(k, c_rstd, c_ssq, c_half, c_bits))
                h0_link(v.tensor_tensor(c_sq[:], c_cen[:], chunk(c_rstd[:]), ALU.mult))
                v.tensor_scalar(h_all[:, c * CH:(c + 1) * CH, :], c_sq[:], 0.0, None, ALU.max).then_inc(h0_ready, 1)
                dve.wait_ge(h0_ready, c + 1)

            cs = [3]

            def chk_link(ins):
                cs[0] += 1
                ins.then_inc(chk_step, 1)
                dve.wait_ge(chk_step, cs[0])

            dve.wait_ge(indices_loaded, 48)
            chk_link(v.tensor_copy(dst_f[:], dst_all[:]))
            chk_link(v.tensor_copy(base_f[:], base_all[:]))
            chk_link(v.tensor_copy(limit_f[:], limit_i[:]))
            chk_link(v.tensor_tensor(rel[:, 0:GROUPS, :], dst_f[:].rearrange("p (g t) -> p g t", t=TILES),
                                     base_f[:].unsqueeze(2).to_broadcast([P, GROUPS, TILES]), ALU.subtract))
            chk_link(v.tensor_tensor(step_f[:, 1:GROUPS], base_f[:, 1:GROUPS], base_f[:, 0:GROUPS - 1], ALU.subtract))
            chk_link(v.memset(carry_rel[:, 0:1], -1.0))
            chk_link(v.tensor_scalar(carry_rel[:, 1:GROUPS], step_f[:, 1:GROUPS], part_f[:, 0:1], -1.0,
                                     ALU.subtract, ALU.mult))
            chk_link(v.tensor_copy(carry_rel[:, GROUPS:GROUPS + 1], carry_rel[:, 0:1]))
            chk_link(v.tensor_copy(rel[:, GROUPS:GROUPS + 2, :], rel[:, 0:2, :]))
            chk_link(v.tensor_reduce(chk[:, 0:1], rel[:, 0:GROUPS, :], mybir.AxisListType.XY, ALU.min))
            chk_link(v.tensor_reduce(chk[:, 3:4], rel[:, 0:GROUPS, :], mybir.AxisListType.XY, ALU.max))
            chk_link(v.tensor_reduce(chk[:, 1:2], step_f[:, 1:GROUPS], X, ALU.min))
            chk_link(v.tensor_tensor(limit_f[:], base_f[:, 6:6 + 4 * (ITERS - LAG - 1) + 1:4], limit_f[:], ALU.subtract))
            chk_link(v.tensor_reduce(chk[:, 2:3], limit_f[:], X, ALU.min))
            chk_link(v.tensor_scalar(chk[:, 3:4], chk[:, 3:4], -1.0, float(WIN - 1), ALU.mult, ALU.add))
            chk_link(v.tensor_reduce(chk[:, 6:7], chk[:, 0:4], X, ALU.min))
            v.tensor_scalar(chk[:, 7:8], chk[:, 6:7], 0.0, None, ALU.is_lt).then_inc(bad_ready, 1)
            dve.wait_ge(weights_loaded, 16 * 13)

            def norm_step(k, step, m, y, g, b, last):
                dve.wait_ge(step, m * NORM_STEPS + (k + CREDIT))
                if k == 1:
                    ins = v.tensor_reduce(tot[:], y, X, ALU.add)
                elif k == 2:
                    ins = v.scalar_tensor_tensor(cen[:], pairs(tot[:]), -1.0 / D, y, ALU.mult, ALU.add)
                elif k == 3:
                    ins = v.tensor_tensor(sq[:], cen[:], cen[:], ALU.mult)
                elif k == 4:
                    ins = v.tensor_reduce(ssq[:], sq[:], X, ALU.add)
                elif k < 5 + RSQRT_STEPS:
                    ins = rsqrt_step(k - 5, rstd, ssq, half, bits)
                elif k == 5 + RSQRT_STEPS:
                    ins = v.tensor_tensor(cen[:], cen[:], pairs(rstd[:]), ALU.mult)
                elif k == 6 + RSQRT_STEPS:
                    ins = v.tensor_tensor(cen[:], cen[:], g.unsqueeze(1).to_broadcast([P, PAIR, D]), ALU.mult)
                else:
                    ins = v.tensor_tensor(last, cen[:], b.unsqueeze(1).to_broadcast([P, PAIR, D]), ALU.add)
                return ins.then_inc(step, 1)

            def divide_sums(m):
                dve.wait_ge(nsum_loaded, 16 * (m + 1))
                v.tensor_scalar(zrec[:], nsum[:, :, D:SW], 1e-6, None, ALU.add).then_inc(divide_step, 1)
                dve.wait_ge(divide_step, done(DIVIDE_STEPS * m))
                v.reciprocal(zrec[:], zrec[:]).then_inc(divide_step, 1)
                dve.wait_ge(divide_step, done(DIVIDE_STEPS * m + 1))
                v.tensor_tensor(attn[:].rearrange("p w (h d) -> p w h d", h=H),
                                nsum[:, :, 0:D].rearrange("p w (h d) -> p w h d", h=H),
                                zrec[:].unsqueeze(3).to_broadcast([P, PAIR, H, DH]), ALU.mult).then_inc(attn_ready, 1)

            def first_norm(l, j, m, steps):
                for k in steps:
                    if k == 0:
                        dve.wait_ge(attn_projected, done(m))
                        v.tensor_tensor(res[:], no_bank[:, 0:PAIR * D].rearrange("p (w d) -> p w d", w=PAIR),
                                        h_all[:, bass.ds(j * PAIR, PAIR), :], ALU.add).then_inc(attn_used, 1)
                        dve.wait_ge(attn_used, done(m))
                        dve.sem_inc(norm1_step, 1)
                    elif k < NORM_STEPS - 1:
                        norm_step(k, norm1_step, m, res[:], norm_sb[:, l, 0, :], norm_sb[:, l, 1, :], h1[:])
                    elif k == NORM_STEPS - 1:
                        dve.wait_ge(norm1_step, m * NORM_STEPS + (k + CREDIT))
                        dve.sem_inc(norm1_step, 1)
                        dve.sem_inc(h1_ready, 1)

            def second_norm(l, j, m, steps):
                xw = x_all[:, bass.ds(j * PAIR, PAIR), :]
                for k in steps:
                    if k == 0:
                        dve.wait_ge(ffn_ready, done(m))
                        v.tensor_tensor(res[:], ffn.rearrange("p (w d) -> p w d", w=PAIR), h1[:], ALU.add)\
                            .then_inc(norm2_step, 1)
                    elif k < NORM_STEPS - 1:
                        norm_step(k, norm2_step, m, res[:], norm_sb[:, l, 2, :], norm_sb[:, l, 3, :],
                                  h2[:] if l + 1 < L else sq[:])
                    elif k == NORM_STEPS - 1:
                        dve.wait_ge(norm2_step, m * NORM_STEPS + (k + CREDIT))
                        if l + 1 < L:
                            dve.sem_inc(h2_ready, 1)
                            v.tensor_scalar(h_all[:, bass.ds(j * PAIR, PAIR), :], h2[:], 1.0, None, ALU.mult)\
                                .then_inc(norm2_step, 1)
                        else:
                            v.tensor_tensor(xw, sq[:], xw, ALU.add).then_inc(norm2_step, 1)
                            dve.wait_ge(norm2_step, m * NORM_STEPS + (k + CREDIT + 1))
                            dve.sem_inc(h2_ready, 1)

            def split_q(b, first=False):
                def step(k, ins):
                    ins.then_inc(split_step, 1)
                    dve.wait_ge(split_step, b * SPLIT_STEPS + (k + CREDIT + 1))
                dve.wait_ge(kvq_staged, done(b))
                if not first:
                    dve.wait_ge(q_stored, 16 * b)
                q = kvq[:, :, 2 * D:3 * D]
                step(0, v.tensor_copy(q_split[:, :, 0:D], q))
                step(1, v.tensor_tensor(q_rest[:], q, q_split[:, :, 0:D], ALU.subtract))
                step(2, v.tensor_copy(q_split[:, :, D:2 * D], q_rest[:]))
                v.tensor_tensor(q_split[:, :, 2 * D:3 * D], q_rest[:], q_split[:, :, D:2 * D], ALU.subtract)\
                    .then_inc(q_split_ready, 1)

            def stage_src(g, s):
                v.tensor_copy(src_slot[:, s % RING, :], src_all[:, bass.ds(g * TILES, TILES)]).then_inc(src_staged, 1)

            def build_onehot(g, s, n):
                dve.wait_ge(group_summed, done(n - RING))
                v.tensor_tensor(onehot[:, s % RING], iota_ps.unsqueeze(1).to_broadcast([P, TILES, WIN]),
                                rel[:, bass.ds(g, 1), :].rearrange("p a t -> p (a t)").unsqueeze(2)
                                .to_broadcast([P, TILES, WIN]), ALU.is_equal).then_inc(onehot_built, 1)

            def build_carry_onehot(g, s):
                v.tensor_scalar(carry_onehot[:, s % RING, :], iota_ps[0:WIN], carry_rel[0:WIN, bass.ds(g, 1)], None,
                                ALU.is_equal).then_inc(carry_onehot_built, 1)

            def use_keys(l, i, s, n):
                dve.wait_ge(kv_gathered[s], 16 * TILES * (l * ITERS + i + 1))
                dve.wait_ge(edge_projected, done(n))
                v.tensor_tensor(prod[:], kv[:, s, :, 0:D], e_bank[:], ALU.mult).then_inc(key_used, 1)

            def use_queries(n):
                dve.wait_ge(query_spread, done(n))
                dve.wait_ge(key_used, done(n))
                v.tensor_tensor(prod[:], prod[:], q_bank[:], ALU.mult).then_inc(query_used, 1)

            def logits(n):
                dve.wait_ge(query_used, done(n))
                v.tensor_reduce(logit[:], prod[:].rearrange("p t (h d) -> p (t h) d", h=H), X, ALU.add)\
                    .then_inc(logit_ready, 1)

            def clip_logits(n):
                dve.wait_ge(logit_ready, done(n))
                v.tensor_scalar(clip[:], logit[:], -5.0 * DH ** 0.5, 5.0 * DH ** 0.5, ALU.max, ALU.min)\
                    .then_inc(clip_ready, 1)

            def messages(s, n):
                dve.wait_ge(score_ready, done(n))
                v.tensor_tensor(msg[:, :, 0:D].rearrange("p t (h d) -> p t h d", h=H),
                                kv[:, s, :, D:2 * D].rearrange("p t (h d) -> p t h d", h=H),
                                msg[:, :, D:SW].unsqueeze(3).to_broadcast([P, TILES, H, DH]),
                                ALU.mult).then_inc(msg_ready, 1)

            def msg_rest_of(s, n):
                dve.wait_ge(msg_hi_ready, done(n))
                v.tensor_tensor(msg_rest[:], msg[:], msg3[:, s % 2, 0], ALU.subtract).then_inc(msg_rest_ready, 1)

            def msg_lo(s, n):
                dve.wait_ge(msg_mid_ready, done(n))
                v.tensor_tensor(msg3[:, s % 2, 2], msg_rest[:], msg3[:, s % 2, 1], ALU.subtract)\
                    .then_inc(msg_lo_ready, 1)

            def take_h0(j):
                v.tensor_copy(h2[:], h_all[:, bass.ds(j * PAIR, PAIR), :]).then_inc(h2_ready, 1)

            take_h0(0)
            split_q(0, first=True)
            with dve.Fori(1, ITERS) as j:
                take_h0(j)
                split_q(j)

            dve.wait_ge(bad_summed, 1)
            v.tensor_copy(flag[:], nt_bank[0:1, 0:1]).then_inc(flag_ready, 1)
            dve.wait_ge(flag_ready, 1)
            bad = dve.value_load(flag[0:1, 0:1], min_val=0, max_val=P)
            with dve.If(bad < 1):
                for s in range(IDX_AHEAD):
                    v.tensor_copy(src_slot[:, s, :], src_all[:, s * TILES:(s + 1) * TILES]).then_inc(src_staged, 1)
                build_onehot(0, 0, 0)
                build_onehot(1, 1, 1)
                build_carry_onehot(0, 0)
                for l in range(L):
                    def one_pass(i, edges=True, first_half=True, second_half=True):
                        m = l * ITERS + i - LAG
                        b = m - 1
                        for s in range(RING):
                            n = l * GROUPS + 4 * i + s

                            def norms(steps):
                                if second_half and s == 1:
                                    second_norm(l, i - LAG - 1, b, steps)
                                if first_half and s == 2:
                                    first_norm(l, i - LAG, m, steps)

                            if edges:
                                use_keys(l, i, s, n)
                                norms(range(0, 2))
                                use_queries(n)
                                norms(range(2, 3))
                                logits(n)
                                norms(range(3, 4))
                                clip_logits(n)
                                norms(range(4, 5))
                                build_onehot(4 * i + s + 2, s + 2, n + 2)
                                norms(range(5, 7))
                                messages(s, n)
                                stage_src(4 * i + s + IDX_AHEAD, s + IDX_AHEAD)
                                norms(range(7, 9))
                                build_carry_onehot(4 * i + s + 1, s + 1)
                                norms(range(9, 12))
                                msg_rest_of(s, n)
                                norms(range(12, 16))
                                msg_lo(s, n)
                                norms(range(16, NORM_STEPS))
                            else:
                                norms(range(NORM_STEPS))
                            if first_half and s == 0:
                                divide_sums(m)
                            if second_half and s == 3 and l + 1 < L:
                                split_q(b + ITERS)

                    for i in range(LAG):
                        one_pass(i, first_half=False, second_half=False)
                    one_pass(LAG, second_half=False)
                    with dve.Fori(LAG + 1, ITERS) as i:
                        one_pass(i)
                    one_pass(ITERS, edges=False)
                    one_pass(ITERS + 1, edges=False)
                    one_pass(ITERS + 2, edges=False, first_half=False)
            with dve.Else():
                for l in range(L):
                    with dve.Fori(0, EDGE_TILES) as t:
                        n = l * EDGE_TILES + t

                        def step(k, ins):
                            ins.then_inc(g_step, 1)
                            dve.wait_ge(g_step, n * G_STEPS + (k + 1))

                        step(0, v.tensor_copy(g_src[:], src_all[:, bass.ds(t, 1)]))
                        step(1, v.tensor_copy(g_dst[:], dst_all[:, bass.ds(t, 1)]))
                        step(2, v.tensor_copy(g_dstf[:], dst_f[:, bass.ds(t, 1)]))
                        v.tensor_copy(g_bc[:], g_dstf[:].to_broadcast([P, P])).then_inc(g_indexed, 1)
                        dve.wait_ge(g_projected, n + 1)
                        step(3, v.tensor_scalar(g_same[:], acc_bank[:, 0:P], g_dstf[:, 0:1], None, ALU.is_equal))
                        step(4, v.tensor_tensor(g_tmp[:], g_same[:], below[:], ALU.mult))
                        step(5, v.tensor_reduce(g_dup[:, 0:1], g_tmp[:], X, ALU.max))
                        step(6, v.tensor_tensor(g_dup[:, 1:2], dump_f[:], g_dstf[:], ALU.subtract))
                        step(7, v.tensor_tensor(g_dup[:, 1:2], g_dup[:, 1:2], g_dup[:, 0:1], ALU.mult))
                        step(8, v.tensor_tensor(g_to[:], g_dup[:, 1:2], g_dstf[:], ALU.add))
                        dve.wait_ge(g_gathered[l], 32 * (t + 1))
                        step(9, v.tensor_tensor(g_q[:], g_q3[:, 0:D], g_q3[:, D:2 * D], ALU.add))
                        step(10, v.tensor_tensor(g_q[:], g_q[:], g_q3[:, 2 * D:3 * D], ALU.add))
                        v.tensor_tensor(prod[:, 0, :], g_kv[:, 0:D], e_bank[:, 0, :], ALU.mult).then_inc(key_used, 1)
                        dve.wait_ge(key_used, done(n))
                        v.tensor_tensor(prod[:, 0, :], prod[:, 0, :], g_q[:], ALU.mult).then_inc(query_used, 1)
                        dve.wait_ge(query_used, done(n))
                        v.tensor_reduce(logit[:, 0:H], prod[:, 0, :].rearrange("p (h d) -> p h d", h=H), X, ALU.add)\
                            .then_inc(logit_ready, 1)
                        dve.wait_ge(logit_ready, done(n))
                        v.tensor_scalar(clip[:, 0:H], logit[:, 0:H], -5.0 * DH ** 0.5, 5.0 * DH ** 0.5, ALU.max, ALU.min)\
                            .then_inc(g_clipped, 1)
                        dve.wait_ge(g_scored, n + 1)
                        v.tensor_tensor(g_msg[:, 0:D].rearrange("p (h d) -> p h d", h=H),
                                        g_kv[:, D:2 * D].rearrange("p (h d) -> p h d", h=H),
                                        g_msg[:, D:SW].unsqueeze(2).to_broadcast([P, H, DH]), ALU.mult)\
                            .then_inc(g_msg_ready, 1)
                        dve.wait_ge(g_summed, n + 1)
                        v.tensor_copy(g_sum[:], q_bank[:].rearrange("p t d -> p (t d)")[:, 0:SW]).then_inc(g_sum_ready, 1)
                        dve.wait_ge(g_added[l], 16 * (t + 1))
                    with dve.Fori(0, ITERS) as j:
                        m = l * ITERS + j
                        divide_sums(m)
                        first_norm(l, j, m, range(NORM_STEPS))
                        second_norm(l, j, m, range(NORM_STEPS))
                        if l + 1 < L:
                            split_q(m + ITERS)


_WEIGHTS = ("WE", "WO", "bO", "ln1_g", "ln1_b", "W1", "b1", "W2", "b2", "ln2_g", "ln2_b")


def kernel(**inputs):
    import concourse.bacc as _bacc
    from concourse.bass_utils import run_bass_kernel_spmd as _run

    def get(name):
        return np.asarray(inputs[name])

    x = np.zeros((NP_, D), np.float32)
    x[:N] = get("x")
    x = x.reshape(WINDOWS, P, D).transpose(1, 0, 2)
    src = np.zeros(EP, np.int32)
    src[:E] = get("src")
    src = src.reshape(EDGE_TILES, P).T
    src = np.concatenate([src, src[:, :IDX_AHEAD * TILES]], axis=1)
    dst = np.full(EP, NP_ - 1, np.int32)
    dst[:E] = get("dst")
    base = dst[::GE]
    dst = dst.reshape(EDGE_TILES, P).T
    attr = np.zeros((EP, D), np.float32)
    attr[:E] = get("edge_attr_64")
    attr = attr.reshape(GROUPS, 2, GE // 2, D).transpose(0, 1, 3, 2)
    wkvq = np.concatenate([get("L0_gnn_WK"), get("L0_gnn_WV"), get("L0_gnn_WQ")], axis=2)
    w = {k: get("L0_gnn_" + k) for k in _WEIGHTS}
    w["b1"] = w["b1"].T
    arrays = dict(x=x, src=src, dst=dst, base=base, edge_attr_t=attr, wkvq=wkvq, we=w["WE"], wo=w["WO"], bo=w["bO"],
                  g1=w["ln1_g"], be1=w["ln1_b"], w1=w["W1"], b1=w["b1"], w2=w["W2"], b2=w["b2"], g2=w["ln2_g"],
                  be2=w["ln2_b"])

    nc = _bacc.Bacc("TRN2", target_bir_lowering=False, num_devices=1)
    maps, aps = {}, {}
    for name, a in arrays.items():
        a = np.ascontiguousarray(a)
        maps[f"in_{name}"] = a
        aps[name] = nc.dram_tensor(f"in_{name}", a.shape, mybir.dt.from_np(a.dtype), kind="ExternalInput").ap()
    aps["out"] = nc.dram_tensor("out_nodes", (P, WINDOWS, D), F32, kind="ExternalOutput").ap()
    gnn(nc, **aps)
    r = _run(nc, [maps], core_ids=[0])
    got = np.asarray(r.results[0]["out_nodes"])
    return got.transpose(1, 0, 2).reshape(NP_, D)[:N]
```

```python
from contextlib import ExitStack

import numpy as np
import concourse.bass as bass
from concourse import mybir

F32 = mybir.dt.float32
BF16 = mybir.dt.bfloat16
I32 = mybir.dt.int32
ALU = mybir.AluOpType
ACT = mybir.ActivationFunctionType
X = mybir.AxisListType.X

P = 128
N, E, D, H, L = 12500, 200000, 64, 4, 2
DH = D // H
HID = 2 * D
EPS = 1e-5
TILES = 8
RING = 4
PAIR = 2
GE = TILES * P
ITERS = -(-E // (RING * GE))
GROUPS = ITERS * RING
EDGE_TILES = GROUPS * TILES
EP = GROUPS * GE
WINDOWS = PAIR * ITERS
ITEMS = ITERS - 1
LAST = ITEMS - 1
QUAD = 2 * PAIR
CH = 14
CHUNKS = WINDOWS // CH
HALVES = ((0, 8), (8, 6))
assert WINDOWS % CH == 0
NP_ = WINDOWS * P
assert NP_ >= N and GROUPS % 2 == 0
LAG = 2
WIN = 80
Q_ROWS = NP_ + P
DUMP = NP_ + P
S_ROWS = NP_ + 2 * P
SW = D + H
CREDIT = 4
NEWTON = 3
RSQRT_MAGIC = float(0x5F3759DF)
GATHER_PASSES = 6
assert (ITERS - 1) % GATHER_PASSES == 0
LAST_TILES = -(-E // P) - (GROUPS - 1) * TILES
assert 0 < LAST_TILES <= TILES
IDX_AHEAD = RING


def done(n):
    return n + (CREDIT + 1)


def gnn(nc, x, src, dst, base, edge_attr_t, wkvq, we, wo, bo, g1, be1, w1, b1, w2, b2, g2, be2, out):
    ctx = ExitStack()
    with ctx:
        def sb(name, shape, dt=F32):
            return ctx.enter_context(nc.sbuf_tensor(name, shape, dt))

        def bank(name, shape, dt=F32):
            return ctx.enter_context(nc.psum_tensor(name, shape, dt))

        def sem(name):
            return ctx.enter_context(nc.semaphore(name))

        kv_table = [nc.dram_tensor(f"kv_table{l}", (NP_, 2 * D), F32).ap() for l in range(L)]
        q_table = [nc.dram_tensor(f"q_table{l}", (Q_ROWS, 3 * D), BF16).ap() for l in range(L)]
        sums = [nc.dram_tensor(f"sums{l}", (S_ROWS, SW), F32).ap() for l in range(L)]

        x_all = sb("x_all", [P, WINDOWS, D])
        h_all = sb("h_all", [P, WINDOWS, D])
        src_all = sb("src_all", [P, (GROUPS + IDX_AHEAD) * TILES], I32)
        dst_all = sb("dst_all", [P, EDGE_TILES], I32)
        base_all = sb("base_all", [P, GROUPS], I32)
        rel = sb("rel", [P, GROUPS + 2, TILES])
        carry_rel = sb("carry_rel", [P, GROUPS + 1])
        src_slot = sb("src_slot", [P, RING, TILES], I32)
        kv = sb("kv", [P, RING, TILES, 2 * D])
        attr = sb("attr", [2 * D, RING, GE // 2])
        q_win = sb("q_win", [WIN, 2, 3 * D], BF16)
        onehot = sb("onehot", [P, RING, TILES, WIN], BF16)
        onehot_t = sb("onehot_t", [WIN, 2, TILES, P], BF16)
        carry_onehot = sb("carry_onehot", [WIN, RING, WIN])
        prod = sb("prod", [P, TILES, D])
        logit = sb("logit", [P, TILES * H])
        clip = sb("clip", [P, TILES * H])
        msg = sb("msg", [P, TILES, SW])
        msg_rest = sb("msg_rest", [P, TILES, SW])
        msg3 = sb("msg3", [P, 2, 3, TILES, SW], BF16)
        carry = sb("carry", [WIN, 2, SW])
        nsum = sb("nsum", [P, QUAD, SW])
        zrec = sb("zrec", [P, QUAD, H])
        attn = sb("attn", [P, QUAD, D])
        attn_t = sb("attn_t", [D + 1, QUAD * P])
        res = sb("res", [P, QUAD, D])
        cen = sb("cen", [P, QUAD, D])
        sq = sb("sq", [P, QUAD, D])
        tot = sb("tot", [P, QUAD])
        ssq = sb("ssq", [P, QUAD])
        rstd = sb("rstd", [P, QUAD])
        half = sb("half", [P, QUAD])
        bits = sb("bits", [P, QUAD], I32)
        h1 = sb("h1", [P, QUAD, D])
        h1_b = sb("h1_b", [P, QUAD, D])
        h1_t = sb("h1_t", [D, QUAD * P])
        hid = sb("hid", [HID, QUAD * P])
        h2 = sb("h2", [P, QUAD, D])
        h2_t = sb("h2_t", [D, QUAD * P])
        kvq = sb("kvq", [P, QUAD, 3 * D])
        q_rest = sb("q_rest", [P, QUAD, D])
        q_split = sb("q_split", [P, QUAD, 3 * D], BF16)
        c_h = sb("c_h", [P, CH, D])
        c_h_t = sb("c_h_t", [2 * D, CH // 2 * P])
        c_split = sb("c_split", [P, CH, 3 * D], BF16)
        c_kvq = kv[:].rearrange("p s t c -> p (s t c)")[:, 0:CH * 3 * D].rearrange("p (w c) -> p w c", w=CH)
        c_rest = attr[:].rearrange("p s e -> p (s e)")[:, 0:CH * D].rearrange("p (w c) -> p w c", w=CH)
        c_cen = sb("c_cen", [P, CH, D])
        c_sq = sb("c_sq", [P, CH, D])
        c_tot = sb("c_tot", [P, CH])
        c_ssq = sb("c_ssq", [P, CH])
        c_rstd = sb("c_rstd", [P, CH])
        c_half = sb("c_half", [P, CH])
        c_bits = sb("c_bits", [P, CH], I32)
        wkvq_sb = sb("wkvq_sb", [2 * D, L, 6 * D])
        we_sb = sb("we_sb", [2 * D, L, 2 * D])
        wo_sb = sb("wo_sb", [D + 1, L, D])
        w1_sb = sb("w1_sb", [D, L, HID])
        b1_sb = sb("b1_sb", [HID, L])
        w2_sb = sb("w2_sb", [HID, L, D])
        b2_sb = sb("b2_sb", [P, L, D])
        norm_sb = sb("norm_sb", [P, L, 4, D])
        ones = sb("ones", [P, P])
        ident = sb("ident", [P, P])
        ident_b = sb("ident_b", [P, P], BF16)
        iota_i = sb("iota_i", [P, P], I32)
        part_i = sb("part_i", [P, 1], I32)
        iota_f = sb("iota_f", [P, P])
        part_f = sb("part_f", [P, 1])
        dump_f = sb("dump_f", [P, 1])
        below = sb("below", [P, P])
        zeros = sb("zeros", [P, S_ROWS // P * SW // 4])
        chk = sb("chk", [P, 8])
        step_f = sb("step_f", [P, GROUPS])
        base_f = sb("base_f", [P, GROUPS])
        limit_i = sb("limit_i", [P, ITERS - LAG], I32)
        limit_f = sb("limit_f", [P, ITERS - LAG])
        dst_f = sb("dst_f", [P, EDGE_TILES])
        flag = sb("flag", [1, 1], I32)
        g_src = sb("g_src", [P, 1], I32)
        g_dst = sb("g_dst", [P, 1], I32)
        g_to = sb("g_to", [P, 1], I32)
        g_dstf = sb("g_dstf", [P, 1])
        g_kv = sb("g_kv", [P, 2 * D])
        g_q3 = sb("g_q3", [P, 3 * D], BF16)
        g_q = sb("g_q", [P, D])
        g_attr = sb("g_attr", [D, P])
        g_dup = sb("g_dup", [P, 4])
        g_bc = sb("g_bc", [P, P])
        g_same = sb("g_same", [P, P])
        g_tmp = sb("g_tmp", [P, P])
        g_msg = sb("g_msg", [P, SW])
        g_sum = sb("g_sum", [P, SW])

        e_bank = bank("e_bank", [P, TILES, D])
        q_bank = bank("q_bank", [P, TILES, D])
        t_bank = bank("t_bank", [WIN, TILES, P], BF16)
        acc_bank = bank("acc_bank", [P, 512])
        nt_bank = bank("nt_bank", [P, 512])
        hid_bank = bank("hid_bank", [P, 512])
        no_bank = bank("no_bank", [P, 512])
        iota_bank = bank("iota_bank", [P, 512])
        acc = acc_bank[0:WIN, 0:SW]
        iota_ps = iota_bank[:, 0:WIN]
        flat_e_bank = e_bank[:].rearrange("p t d -> p (t d)")
        kvq_banks = (flat_e_bank, q_bank[:].rearrange("p t d -> p (t d)"), hid_bank, no_bank)

        def ffn_of(w):
            return hid_bank[:, PAIR * P:PAIR * P + w * D] if w == PAIR else flat_e_bank[:, 0:w * D]


        weights_loaded = sem("weights_loaded")
        kvq_weights_loaded = sem("kvq_weights_loaded")
        x_loaded = [sem(f"x_loaded{k}") for k in range(2)]
        indices_loaded = sem("indices_loaded")
        attr_loaded = [sem(f"attr_loaded{s}") for s in range(RING)]
        q_win_loaded = [sem(f"q_win_loaded{s}") for s in range(2)]
        kv_gathered = [sem(f"kv_gathered{s}") for s in range(RING)]
        q_pad_zeroed = sem("q_pad_zeroed")
        sums_zeroed = [sem(f"sums_zeroed{l}") for l in range(L)]
        sums_written = sem("sums_written")
        nsum_loaded = sem("nsum_loaded")
        kv_stored = sem("kv_stored")
        q_stored = sem("q_stored")
        out_stored = sem("out_stored")
        pool_consts = sem("pool_consts")
        dve_consts = sem("dve_consts")
        c_step = sem("c_step")
        c_centered = sem("c_centered")
        c_squared = sem("c_squared")
        c_h_ready = sem("c_h_ready")
        c_h_kept = sem("c_h_kept")
        c_turned = sem("c_turned")
        c_h_t_ready = sem("c_h_t_ready")
        c_projected = sem("c_projected")
        c_kvq_ready = sem("c_kvq_ready")
        c_split_step = sem("c_split_step")
        c_split_ready = sem("c_split_ready")
        c_kv_stored = [sem(f"c_kv_stored{k}") for k in range(2)]
        c_q_stored = [sem(f"c_q_stored{k}") for k in range(2)]
        chk_step = sem("chk_step")
        dst_f_ready = sem("dst_f_ready")
        bad_ready = sem("bad_ready")
        bad_summed = sem("bad_summed")
        flag_ready = sem("flag_ready")
        src_staged = sem("src_staged")
        onehot_built = sem("onehot_built")
        carry_onehot_built = sem("carry_onehot_built")
        onehot_turned = sem("onehot_turned")
        onehot_t_ready = sem("onehot_t_ready")
        edge_projected = sem("edge_projected")
        query_spread = sem("query_spread")
        key_used = sem("key_used")
        query_used = sem("query_used")
        logit_ready = sem("logit_ready")
        clip_ready = sem("clip_ready")
        score_ready = sem("score_ready")
        msg_ready = sem("msg_ready")
        msg_hi_ready = sem("msg_hi_ready")
        msg_rest_ready = sem("msg_rest_ready")
        msg_mid_ready = sem("msg_mid_ready")
        msg_lo_ready = sem("msg_lo_ready")
        group_summed = sem("group_summed")
        carry_ready = sem("carry_ready")
        attn_ready = sem("attn_ready")
        attn_turned = sem("attn_turned")
        attn_t_ready = sem("attn_t_ready")
        attn_projected = sem("attn_projected")
        attn_used = sem("attn_used")
        h1_ready = sem("h1_ready")
        h1_turned = sem("h1_turned")
        h1_t_ready = sem("h1_t_ready")
        hid_ready = sem("hid_ready")
        relu_ready = sem("relu_ready")
        ffn_ready = sem("ffn_ready")
        h2_ready = sem("h2_ready")
        h2_turned = sem("h2_turned")
        h2_t_ready = sem("h2_t_ready")
        kvq_projected = sem("kvq_projected")
        kvq_staged = sem("kvq_staged")
        q_split_ready = sem("q_split_ready")
        divide_step = sem("divide_step")
        norm1_step = sem("norm1_step")
        norm2_step = sem("norm2_step")
        split_step = sem("split_step")
        sp_passed = sem("sp_passed")
        pool_passed = sem("pool_passed")
        pe_passed = sem("pe_passed")
        g_indexed = sem("g_indexed")
        g_attr_loaded = sem("g_attr_loaded")
        g_gathered = [sem(f"g_gathered{l}") for l in range(L)]
        g_step = sem("g_step")
        g_projected = sem("g_projected")
        g_clipped = sem("g_clipped")
        g_scored = sem("g_scored")
        g_msg_ready = sem("g_msg_ready")
        g_summed = sem("g_summed")
        g_sum_ready = sem("g_sum_ready")
        g_added = [sem(f"g_added{l}") for l in range(L)]

        ZERO_FILLS = 4
        DIVIDE_STEPS = 2
        RSQRT_STEPS = 4 + 3 * NEWTON
        NORM_STEPS = 1 + 4 + RSQRT_STEPS + 3 + 1
        SPLIT_STEPS = 3
        CHUNK_STEPS = 3 + RSQRT_STEPS
        G_STEPS = 11
        block = ctx.enter_context(nc.Block())

        def window_rows(table, first, w):
            return table[bass.ds(first * P, w * P), :].rearrange("(w p) c -> p w c", p=P)

        @block.sync
        def _(sp):
            sp.dma_start(x_all[:, 0:CH], x[:, 0:CH]).then_inc(x_loaded[0], 16)
            sp.wait_ge(pool_consts, 2)
            for half in range(2):
                sp.dma_start(wkvq_sb[half * D:(half + 1) * D, :, half * 3 * D:(half + 1) * 3 * D],
                             wkvq.rearrange("l k n -> k l n")).then_inc(kvq_weights_loaded, 16)
            sp.dma_start(x_all[:, CH:WINDOWS], x[:, CH:WINDOWS]).then_inc(x_loaded[1], 16)
            sp.dma_start(src_all[:], src).then_inc(indices_loaded, 16)
            sp.dma_start(dst_all[:], dst).then_inc(indices_loaded, 16)
            sp.dma_start(base_all[:], base.partition_broadcast(P)).then_inc(indices_loaded, 16)
            for half in range(2):
                on = slice(half * D, (half + 1) * D)
                sp.dma_start(we_sb[on, :, on], we.rearrange("l k n -> k l n")).then_inc(weights_loaded, 16)
            sp.dma_start(wo_sb[0:D], wo.rearrange("l k n -> k l n")).then_inc(weights_loaded, 16)
            sp.dma_start(wo_sb[D:D + 1], bo.unsqueeze(0)).then_inc(weights_loaded, 16)
            sp.dma_start(w1_sb[:], w1.rearrange("l k n -> k l n")).then_inc(weights_loaded, 16)
            sp.dma_start(b1_sb[:], b1).then_inc(weights_loaded, 16)
            sp.dma_start(w2_sb[:], w2.rearrange("l k n -> k l n")).then_inc(weights_loaded, 16)
            sp.dma_start(b2_sb[:], b2.partition_broadcast(P)).then_inc(weights_loaded, 16)
            for k, a in enumerate((g1, be1, g2, be2)):
                sp.dma_start(norm_sb[:, :, k, :], a.partition_broadcast(P)).then_inc(weights_loaded, 16)
            sp.wait_ge(pool_consts, 3)
            for l in range(L):
                sp.dma_start(q_table[l][NP_:Q_ROWS, :], zeros[:, 0:3 * D // 2].bitcast(BF16)).then_inc(q_pad_zeroed, 16)
            sp.wait_ge(q_pad_zeroed, 16 * L)
            sp.wait_ge(indices_loaded, 48)

            with sp.Fori(0, CHUNKS) as c:
                for half, (w0, w) in enumerate(HALVES):
                    sp.wait_ge(c_kvq_ready, done(c * (CH // 2) + (w0 + w) // 2 - 1))
                    sp.dma_start(window_rows(kv_table[0], c * CH + w0, w), c_kvq[:, w0:w0 + w, 0:2 * D])\
                        .then_inc(c_kv_stored[half], 16)
                for half, (w0, w) in enumerate(HALVES):
                    sp.wait_ge(c_split_ready, done(2 * c + half))
                    sp.dma_start(window_rows(q_table[0], c * CH + w0, w), c_split[:, w0:w0 + w])\
                        .then_inc(c_q_stored[half], 16)

            def zero_sums(l):
                part = S_ROWS // ZERO_FILLS
                for k in range(ZERO_FILLS):
                    sp.dma_start(sums[l][k * part:(k + 1) * part, :].rearrange("(p r) c -> p (r c)", p=P),
                                 zeros[:]).then_inc(sums_zeroed[l], 16)

            def attr_group(g):
                return edge_attr_t[bass.ds(g, 1)].rearrange("a h f e -> (a h f) e")

            def load_group(l, i, s):
                n = l * GROUPS + 4 * i + s
                sp.wait_ge(edge_projected, done(n - RING))
                sp.dma_start(attr[:, s, :], attr_group(4 * i + s)).then_inc(attr_loaded[s], 16)
                first = sp.value_load(base_all[0:1, bass.ds(4 * i + s, 1)], min_val=0, max_val=NP_ - 1)
                sp.wait_ge(query_spread, done(n - 2))
                sp.dma_start(q_win[:, s % 2, :], q_table[l][bass.ds(first, WIN), :]).then_inc(q_win_loaded[s % 2], 16)

            def load_nsum(l, j, written, w=PAIR):
                if written is not None:
                    sp.wait_ge(sums_written, 16 * (written + 1))
                    sp.sem_inc(sp_passed, 1)
                sp.wait_ge(attn_ready, done(l * ITEMS + j - 1))
                sp.dma_start(nsum[:, 0:w], window_rows(sums[l], j * PAIR, w)).then_inc(nsum_loaded, 16)

            def wait_q_table(l):
                if l == 0:
                    for stored in c_q_stored:
                        sp.wait_ge(stored, 16 * (CHUNKS + 1))
                else:
                    sp.wait_ge(q_stored, 16 * (l * ITEMS + 1))

            sp.wait_ge(flag_ready, 1)
            bad = sp.value_load(flag[0:1, 0:1], min_val=0, max_val=P)
            with sp.If(bad < 1):
                for l in range(L):
                    wait_q_table(l)
                    for i in range(LAG):
                        for s in range(RING):
                            load_group(l, i, s)
                        if i == 0:
                            zero_sums(l)
                    with sp.Fori(LAG, ITERS) as i:
                        for s in range(RING):
                            load_group(l, i, s)
                            if s == 0:
                                load_nsum(l, i - LAG, l * GROUPS + 4 * i - 2)
                    load_nsum(l, LAST, (l + 1) * GROUPS, QUAD)
            with sp.Else():
                for l in range(L):
                    zero_sums(l)
                    with sp.Fori(0, EDGE_TILES // 4) as q:
                        for t in range(4):
                            sp.dma_start(g_attr[:], edge_attr_t.rearrange("g h f e -> (g h) f e")[
                                bass.ds(q, 1), :, t * P:(t + 1) * P].rearrange("a f e -> (a f) e"))\
                                .then_inc(g_attr_loaded, 16)
                            sp.wait_ge(g_projected, l * EDGE_TILES + 4 * q + (t + 1))
                            sp.sem_inc(sp_passed, 1)
                    sp.wait_ge(g_added[l], 16 * EDGE_TILES)
                    with sp.Fori(0, LAST) as j:
                        load_nsum(l, j, None)
                    load_nsum(l, LAST, None, QUAD)

        @block.gpsimd
        def _(pool):
            nc.gpsimd.memset(wkvq_sb[:], 0.0).then_inc(pool_consts, 1)
            nc.gpsimd.memset(we_sb[:], 0.0).then_inc(pool_consts, 1)
            nc.gpsimd.memset(zeros[:], 0.0).then_inc(pool_consts, 1)
            nc.gpsimd.memset(ones[:], 1.0).then_inc(pool_consts, 1)
            nc.gpsimd.memset(carry[:], 0.0).then_inc(pool_consts, 1)
            nc.gpsimd.memset(attn_t[:], 1.0).then_inc(pool_consts, 1)
            nc.gpsimd.iota(iota_i[:], [[1, P]], base=0, channel_multiplier=0).then_inc(pool_consts, 1)
            nc.gpsimd.iota(part_i[:], [[0, 1]], base=0, channel_multiplier=1).then_inc(pool_consts, 1)
            nc.gpsimd.iota(limit_i[:], [[PAIR * P, ITERS - LAG]], base=PAIR * P, channel_multiplier=0)\
                .then_inc(pool_consts, 1)

            def wait_kv_table(l):
                if l == 0:
                    for stored in c_kv_stored:
                        pool.wait_ge(stored, 16 * (CHUNKS + 1))
                else:
                    pool.wait_ge(kv_stored, 16 * (l * ITEMS + 1))

            pool.wait_ge(flag_ready, 1)
            bad = pool.value_load(flag[0:1, 0:1], min_val=0, max_val=P)
            with pool.If(bad < 1):
                for l in range(L):
                    wait_kv_table(l)
                    def gather_group(n, s, tiles=TILES):
                        pool.wait_ge(src_staged, done(n))
                        pool.wait_ge(msg_ready, done(n - RING))
                        pool.sem_inc(pool_passed, 1)
                        for t in range(tiles):
                            nc.gpsimd.indirect_dma_start(
                                out=kv[:, s, t, :], out_offset=None, in_=kv_table[l][:, :],
                                in_offset=bass.IndirectOffsetOnAxis(ap=src_slot[:, s, t:t + 1], axis=0),
                            ).then_inc(kv_gathered[s], 16)

                    with pool.Fori(0, (ITERS - 1) // GATHER_PASSES) as trip:
                        for k in range(GATHER_PASSES * RING):
                            gather_group(l * GROUPS + GATHER_PASSES * RING * trip + k, k % RING)
                    for s in range(RING - 1):
                        gather_group((l + 1) * GROUPS - RING + s, s)
                    gather_group((l + 1) * GROUPS - 1, RING - 1, LAST_TILES)
            with pool.Else():
                for l in range(L):
                    wait_kv_table(l)
                    if l == 0:
                        for stored in c_q_stored:
                            pool.wait_ge(stored, 16 * (CHUNKS + 1))
                    else:
                        pool.wait_ge(q_stored, 16 * (l * ITEMS + 1))
                    pool.wait_ge(q_pad_zeroed, 16 * L)
                    pool.wait_ge(sums_zeroed[l], 16 * ZERO_FILLS)
                    with pool.Fori(0, EDGE_TILES) as t:
                        n = l * EDGE_TILES + t
                        pool.wait_ge(g_indexed, n + 1)
                        pool.sem_inc(pool_passed, 1)
                        nc.gpsimd.indirect_dma_start(
                            out=g_kv[:], out_offset=None, in_=kv_table[l][:, :],
                            in_offset=bass.IndirectOffsetOnAxis(ap=g_src[:, 0:1], axis=0)).then_inc(g_gathered[l], 16)
                        nc.gpsimd.indirect_dma_start(
                            out=g_q3[:], out_offset=None, in_=q_table[l][:, :],
                            in_offset=bass.IndirectOffsetOnAxis(ap=g_dst[:, 0:1], axis=0)).then_inc(g_gathered[l], 16)
                        pool.wait_ge(g_sum_ready, n + 1)
                        pool.sem_inc(pool_passed, 1)
                        nc.gpsimd.indirect_dma_start(
                            out=sums[l][:, :], out_offset=bass.IndirectOffsetOnAxis(ap=g_to[:, 0:1], axis=0),
                            in_=g_sum[:], in_offset=None, compute_op=ALU.add).then_inc(g_added[l], 16)
                        pool.wait_ge(g_added[l], 16 * (t + 1))
                        pool.sem_inc(pool_passed, 1)

        @block.tensor
        def _(pe):
            for done_by_pe in (onehot_turned, edge_projected, query_spread, group_summed, attn_turned,
                               attn_projected, h1_turned, hid_ready, ffn_ready, h2_turned, kvq_projected, c_turned,
                               c_projected):
                pe.sem_inc(done_by_pe, CREDIT)

            def turn_attn(m, w):
                pe.wait_ge(attn_ready, done(m))
                pe.sem_inc(pe_passed, 1)
                for k in range(w):
                    last = pe.transpose(nt_bank[0:D, k * P:(k + 1) * P], attn[:, k, :], ident[:])
                last.then_inc(attn_turned, 1)

            def project_attn(l, m, b, w):
                if l + 1 < L:
                    pe.wait_ge(kvq_staged, done(b))
                pe.wait_ge(attn_t_ready, done(m))
                for k in range(w):
                    last = pe.matmul(no_bank[:, k * D:(k + 1) * D], attn_t[:, k * P:(k + 1) * P], wo_sb[:, l, :],
                                     start=True, stop=True)
                last.then_inc(attn_projected, 1)

            def turn_h1(m, w):
                pe.wait_ge(h1_ready, done(m))
                pe.sem_inc(pe_passed, 1)
                for k in range(w):
                    last = pe.transpose(nt_bank[0:D, k * P:(k + 1) * P], h1[:, k, :], ident[:])
                last.then_inc(h1_turned, 1)

            def project_hidden(l, m, w):
                pe.wait_ge(h1_t_ready, done(m))
                pe.matmul(hid_bank[:, 0:w * P], w1_sb[:, l, :], h1_t[:, 0:w * P], start=True, stop=True).then_inc(hid_ready, 1)

            def project_ffn(l, m, w):
                pe.wait_ge(relu_ready, done(m))
                for k in range(w):
                    last = pe.matmul(ffn_of(w)[:, k * D:(k + 1) * D], hid[:, k * P:(k + 1) * P], w2_sb[:, l, :],
                                     start=True, stop=True)
                last.then_inc(ffn_ready, 1)

            def turn_h2(m, w):
                pe.wait_ge(h2_ready, done(m))
                pe.sem_inc(pe_passed, 1)
                for k in range(w):
                    last = pe.transpose(nt_bank[0:D, k * P:(k + 1) * P], h2[:, k, :], ident[:])
                last.then_inc(h2_turned, 1)

            def project_kvq(l, m, a, w):
                pe.wait_ge(h2_t_ready, done(m))
                pe.wait_ge(attn_used, done(a))
                pe.wait_ge(kvq_staged, done(m - 1))
                for k in range(w):
                    o = (no_bank, hid_bank)[k // PAIR][:, (k % PAIR) * 3 * D:(k % PAIR + 1) * 3 * D]
                    last = pe.matmul(o, h2_t[:, k * P:(k + 1) * P], wkvq_sb[0:D, l + 1, 0:3 * D], start=True, stop=True)
                last.then_inc(kvq_projected, 1)

            def turn_onehot(s, n):
                pe.wait_ge(onehot_built, done(n))
                pe.wait_ge(onehot_t_ready, done(n - 1))
                for t in range(TILES):
                    last = pe.transpose(t_bank[:, t, :], onehot[:, s % RING, t, :], ident_b[:])
                last.then_inc(onehot_turned, 1)

            def project_edges(l, i, s, n):
                pe.wait_ge(attr_loaded[s], 16 * (l * ITERS + i + 1))
                pe.wait_ge(key_used, done(n - 1))
                for t in range(TILES // 2):
                    last = pe.matmul(e_bank[:, t::TILES // 2, :], attr[:, s, t * P:(t + 1) * P], we_sb[:, l, :],
                                     start=True, stop=True)
                last.then_inc(edge_projected, 1)

            def spread_query(l, i, s, n):
                pe.wait_ge(onehot_t_ready, done(n))
                pe.wait_ge(q_win_loaded[s % 2], 16 * (2 * (l * ITERS + i) + s // 2 + 1))
                pe.wait_ge(query_used, done(n - 1))
                for t in range(TILES):
                    for k in range(3):
                        last = pe.matmul(q_bank[:, t, :], onehot_t[:, s % 2, t, :], q_win[:, s % 2, k * D:(k + 1) * D],
                                         start=(k == 0), stop=(k == 2))
                last.then_inc(query_spread, 1)

            def sum_group(s, n):
                pe.wait_ge(carry_onehot_built, done(n))
                pe.wait_ge(carry_ready, done(n - 1))
                pe.matmul(acc, carry_onehot[:, s % RING, :], carry[:, (s - 1) % 2, :], start=True, stop=False)
                pe.wait_ge(msg_lo_ready, done(n))
                for t in range(TILES):
                    for k in range(3):
                        last = pe.matmul(acc, onehot[:, s % RING, t, :], msg3[:, s % 2, k, t, :],
                                         start=False, stop=(t == TILES - 1 and k == 2))
                last.then_inc(group_summed, 1)

            pe.wait_ge(dve_consts, 4)
            with pe.Fori(0, CHUNKS) as c:
                pe.wait_ge(c_h_ready, done(c))
                pe.sem_inc(pe_passed, 1)
                for half, (w0, w) in enumerate(HALVES):
                    for k in range(w // 2):
                        last = pe.transpose((nt_bank, acc_bank)[half][:, k * P:(k + 1) * P],
                                            c_h[:, w0 + 2 * k:w0 + 2 * k + 2, :].rearrange("p w d -> p (w d)"), ident[:])
                    last.then_inc(c_turned, 1)
                pe.wait_ge(kvq_weights_loaded, 32)
                for half, (w0, w) in enumerate(HALVES):
                    pe.wait_ge(c_h_t_ready, done(2 * c + half))
                    for k in range(w0 // 2, (w0 + w) // 2):
                        pe.wait_ge(c_kvq_ready, done(c * (CH // 2) + k - 3))
                        pe.matmul(kvq_banks[k % 4][:, 0:6 * D], c_h_t[:, k * P:(k + 1) * P], wkvq_sb[:, 0, :],
                                  start=True, stop=True).then_inc(c_projected, 1)

            pe.wait_ge(weights_loaded, 16 * 12)
            pe.wait_ge(bad_ready, 1)
            pe.matmul(nt_bank[0:1, 0:1], chk[:, 7:8], ones[:, 0:1], start=True, stop=True).then_inc(bad_summed, 1)
            pe.wait_ge(flag_ready, 1)
            bad = pe.value_load(flag[0:1, 0:1], min_val=0, max_val=P)
            with pe.If(bad < 1):
                turn_onehot(0, 0)
                for l in range(L):
                    def one_pass(i, edges=True, first=True, second=True, start=False, last_pass=False,
                                 w=PAIR):
                        m = l * ITEMS + i - LAG
                        b = m - 1
                        wb = PAIR if first else w
                        for s in range(RING):
                            n = l * GROUPS + 4 * i + s
                            if edges:
                                spread_query(l, i, s, n)
                                turn_onehot(s + 1, n + 1)
                                if not (last_pass and s == RING - 1):
                                    project_edges(l, i + (s + 1) // RING, (s + 1) % RING, n + 1)
                            if second and s == 0:
                                turn_h1(b, wb)
                            if second and s == 1:
                                project_ffn(l, b, wb)
                            if first and s == 1:
                                turn_attn(m, w)
                            if second and s == 3 and l + 1 < L:
                                turn_h2(b, wb)
                            if edges and not (start and s == 0):
                                sum_group(s - 1, n - 1)
                            if second and s == 0:
                                project_hidden(l, b, wb)
                                if not edges and first:
                                    sum_group(RING - 1, (l + 1) * GROUPS - 1)
                            if first and s == 1:
                                project_attn(l, m, m - 2, w)
                            if second and s == 3 and l + 1 < L:
                                project_kvq(l, b, m if first else b, wb)

                    project_edges(l, 0, 0, l * GROUPS)
                    one_pass(0, first=False, second=False, start=True)
                    one_pass(1, first=False, second=False)
                    one_pass(2, second=False)
                    with pe.Fori(LAG + 1, ITERS - 1) as i:
                        one_pass(i)
                    one_pass(ITERS - 1, last_pass=True)
                    one_pass(ITERS, edges=False, w=QUAD)
                    one_pass(ITERS + 1, edges=False, first=False, w=QUAD)
            with pe.Else():
                for l in range(L):
                    with pe.Fori(0, EDGE_TILES) as t:
                        n = l * EDGE_TILES + t
                        pe.wait_ge(g_attr_loaded, 16 * (n + 1))
                        pe.wait_ge(g_indexed, n + 1)
                        pe.matmul(e_bank[:, 0, :], g_attr[:], we_sb[0:D, l, 0:D], start=True, stop=True)
                        pe.transpose(acc_bank[:, 0:P], g_bc[:], ident[:]).then_inc(g_projected, 1)
                        pe.wait_ge(g_msg_ready, n + 1)
                        pe.matmul(q_bank[:].rearrange("p t d -> p (t d)")[:, 0:SW], g_same[:], g_msg[:],
                                  start=True, stop=True).then_inc(g_summed, 1)

                    def one_item(m, w):
                        turn_attn(m, w)
                        project_attn(l, m, m - 1, w)
                        turn_h1(m, w)
                        project_hidden(l, m, w)
                        project_ffn(l, m, w)
                        if l + 1 < L:
                            turn_h2(m, w)
                            project_kvq(l, m, m, w)

                    with pe.Fori(0, LAST) as j:
                        one_item(l * ITEMS + j, PAIR)
                    one_item(l * ITEMS + LAST, QUAD)

        @block.scalar
        def _(act):
            for done_by_act in (onehot_t_ready, score_ready, msg_hi_ready, msg_mid_ready, carry_ready, attn_t_ready, h1_t_ready,
                                relu_ready, h2_t_ready, kvq_staged, c_squared, c_h_kept, c_h_t_ready, c_kvq_ready):
                act.sem_inc(done_by_act, CREDIT)
            act.sem_inc(kv_stored, 16)
            act.sem_inc(sums_written, 16)

            def copy_attn_t(m, w):
                act.wait_ge(attn_turned, done(m))
                nc.scalar.copy(attn_t[0:D, 0:w * P], nt_bank[0:D, 0:w * P]).then_inc(attn_t_ready, 1)

            def copy_h1_t(m, w):
                act.wait_ge(h1_turned, done(m))
                nc.scalar.copy(h1_t[:, 0:w * P], nt_bank[0:D, 0:w * P]).then_inc(h1_t_ready, 1)

            def relu_hidden(l, m, w):
                act.wait_ge(hid_ready, done(m))
                nc.scalar.activation(hid[:, 0:w * P], hid_bank[:, 0:w * P], ACT.Relu, bias=b1_sb[:, l:l + 1])\
                    .then_inc(relu_ready, 1)

            def copy_h2_t(m, w):
                act.wait_ge(h2_turned, done(m))
                nc.scalar.copy(h2_t[:, 0:w * P], nt_bank[0:D, 0:w * P]).then_inc(h2_t_ready, 1)

            def store_kv(l, j, m, w):
                act.wait_ge(kvq_projected, done(m))
                act.wait_ge(q_split_ready, done(m - 1))
                act.wait_ge(kv_stored, 16 * (m + 1))
                for k in range(w // PAIR):
                    last = nc.scalar.copy(kvq[:, k * PAIR:(k + 1) * PAIR, :].rearrange("p w c -> p (w c)"),
                                          (no_bank, hid_bank)[k][:, 0:PAIR * 3 * D])
                last.then_inc(kvq_staged, 1)
                act.wait_ge(kvq_staged, done(m))
                act.dma_start(window_rows(kv_table[l + 1], j * PAIR, w), kvq[:, 0:w, 0:2 * D]).then_inc(kv_stored, 16)

            def store_q(l, j, m, w):
                act.wait_ge(q_split_ready, done(m))
                act.dma_start(window_rows(q_table[l + 1], j * PAIR, w), q_split[:, 0:w]).then_inc(q_stored, 16)

            def store_out(j, m, w):
                act.wait_ge(h2_ready, done(m))
                act.dma_start(out[:, bass.ds(j * PAIR, w), :], x_all[:, bass.ds(j * PAIR, w), :]).then_inc(out_stored, 16)

            def copy_onehot_t(s, n):
                act.wait_ge(onehot_turned, done(n))
                nc.scalar.copy(onehot_t[:, s % 2], t_bank[:]).then_inc(onehot_t_ready, 1)

            def exp_scores(s, n):
                act.wait_ge(clip_ready, done(n))
                nc.scalar.activation(msg[:, :, D:SW], clip[:].rearrange("p (t h) -> p t h", h=H), ACT.Exp,
                                     scale=DH ** -0.5).then_inc(score_ready, 1)

            def msg_hi(s, n):
                act.wait_ge(msg_ready, done(n))
                nc.scalar.copy(msg3[:, s % 2, 0], msg[:]).then_inc(msg_hi_ready, 1)

            def msg_mid(s, n):
                act.wait_ge(msg_rest_ready, done(n))
                nc.scalar.copy(msg3[:, s % 2, 1], msg_rest[:]).then_inc(msg_mid_ready, 1)

            def write_sums(l, g, s, n, first_write=False):
                act.wait_ge(group_summed, done(n))
                nc.scalar.copy(carry[:, s % 2, :], acc).then_inc(carry_ready, 1)
                first = act.value_load(base_all[0:1, bass.ds(g, 1)], min_val=0, max_val=NP_ - 1)
                if first_write:
                    act.wait_ge(sums_zeroed[l], 16 * ZERO_FILLS)
                act.wait_ge(sums_written, 16 * (n + 1))
                act.wait_ge(carry_ready, done(n))
                act.dma_start(sums[l][bass.ds(first, WIN), :], carry[:, s % 2, :]).then_inc(sums_written, 16)

            def square(c):
                act.wait_ge(c_centered, done(c))
                nc.scalar.square(c_sq[:], c_cen[:]).then_inc(c_squared, 1)

            def keep_h(c):
                act.wait_ge(c_h_ready, done(c))
                nc.scalar.copy(h_all[:, bass.ds(c * CH, CH), :], c_h[:]).then_inc(c_h_kept, 1)

            def copy_half_t(c, half):
                w0, w = HALVES[half]
                act.wait_ge(c_turned, done(2 * c + half))
                nc.scalar.copy(c_h_t[:, w0 // 2 * P:(w0 + w) // 2 * P], (nt_bank, acc_bank)[half][:, 0:w // 2 * P])\
                    .then_inc(c_h_t_ready, 1)

            def stage_chunk(c):
                for half, (w0, w) in enumerate(HALVES):
                    act.wait_ge(c_split_ready, done(2 * (c - 1) + half))
                    act.wait_ge(c_kv_stored[half], 16 * (c + 1))
                    for k in range(w0 // 2, (w0 + w) // 2):
                        act.wait_ge(c_projected, done(c * (CH // 2) + k))
                        nc.scalar.copy(c_kvq[:, 2 * k:2 * k + 2, :].rearrange("p w c -> p (w c)"),
                                       kvq_banks[k % 4][:, 0:6 * D]).then_inc(c_kvq_ready, 1)

            for stored in c_kv_stored:
                act.sem_inc(stored, 16)
            square(0)
            with act.Fori(0, CHUNKS - 1) as c:
                keep_h(c)
                copy_half_t(c, 0)
                square(c + 1)
                copy_half_t(c, 1)
                stage_chunk(c)
            act.wait_ge(indices_loaded, 48)
            nc.scalar.copy(dst_f[:], dst_all[:]).then_inc(dst_f_ready, 1)
            copy_half_t(CHUNKS - 1, 0)
            copy_half_t(CHUNKS - 1, 1)
            stage_chunk(CHUNKS - 1)
            keep_h(CHUNKS - 1)

            act.wait_ge(flag_ready, 1)
            bad = act.value_load(flag[0:1, 0:1], min_val=0, max_val=P)
            with act.If(bad < 1):
                copy_onehot_t(0, 0)

                for l in range(L):
                    def one_pass(i, edges=True, first=True, second=True, third=True, start=False, w=PAIR):
                        m = l * ITEMS + i - LAG
                        b, q = m - 1, m - 2
                        wb = PAIR if first else w
                        wq = PAIR if second else w
                        for s in range(RING):
                            n = l * GROUPS + 4 * i + s
                            if edges:
                                copy_onehot_t(s + 1, n + 1)
                                if not (start and s == 0):
                                    msg_mid(s - 1, n - 1)
                                exp_scores(s, n)
                            if not edges and first and s == 0:
                                msg_mid(RING - 1, (l + 1) * GROUPS - 1)
                            if second and s == 0:
                                copy_h1_t(b, wb)
                            if third and s == 1 and l + 1 < L:
                                store_q(l, i - LAG - 2, q, wq)
                            if first and s == 1:
                                copy_attn_t(m, w)
                            if second and s == 3 and l + 1 < L:
                                copy_h2_t(b, wb)
                            if edges:
                                msg_hi(s, n)
                                if not (start and s == 0):
                                    write_sums(l, 4 * i + s - 1, s - 1, n - 1, start and s == 1)
                            if second and s == 0:
                                relu_hidden(l, b, wb)
                                if not edges and first:
                                    write_sums(l, GROUPS - 1, RING - 1, (l + 1) * GROUPS - 1)
                            if second and s == 3:
                                if l + 1 < L:
                                    store_kv(l, i - LAG - 1, b, wb)
                                else:
                                    store_out(i - LAG - 1, b, wb)

                    one_pass(0, first=False, second=False, third=False, start=True)
                    one_pass(1, first=False, second=False, third=False)
                    one_pass(2, second=False, third=False)
                    one_pass(3, third=False)
                    with act.Fori(LAG + 2, ITERS) as i:
                        one_pass(i)
                    one_pass(ITERS, edges=False, w=QUAD)
                    one_pass(ITERS + 1, edges=False, first=False, w=QUAD)
                    one_pass(ITERS + 2, edges=False, first=False, second=False, w=QUAD)
                act.wait_ge(sums_written, 16 * (L * GROUPS + 1))
            with act.Else():
                for l in range(L):
                    with act.Fori(0, EDGE_TILES) as t:
                        n = l * EDGE_TILES + t
                        act.wait_ge(g_clipped, n + 1)
                        nc.scalar.activation(g_msg[:, D:SW], clip[:, 0:H], ACT.Exp, scale=DH ** -0.5).then_inc(g_scored, 1)

                    def one_item(j, m, w):
                        copy_attn_t(m, w)
                        copy_h1_t(m, w)
                        relu_hidden(l, m, w)
                        if l + 1 < L:
                            copy_h2_t(m, w)
                            store_kv(l, j, m, w)
                            store_q(l, j, m, w)
                        else:
                            store_out(j, m, w)

                    with act.Fori(0, LAST) as j:
                        one_item(j, l * ITEMS + j, PAIR)
                    one_item(LAST, l * ITEMS + LAST, QUAD)
            act.wait_ge(out_stored, 16 * ITEMS)
            act.wait_ge(kv_stored, 16 * ((L - 1) * ITEMS + 1))
            act.wait_ge(q_stored, 16 * ((L - 1) * ITEMS + 1))

        @block.vector
        def _(dve):
            v = nc.vector
            for done_by_dve in (src_staged, onehot_built, carry_onehot_built, key_used, query_used, logit_ready,
                                clip_ready, msg_ready, msg_rest_ready, msg_lo_ready, attn_ready, attn_used, h1_ready,
                                h2_ready, q_split_ready, divide_step, norm1_step, norm2_step, split_step, c_step, c_centered, c_h_ready, c_split_step,
                                c_split_ready):
                dve.sem_inc(done_by_dve, CREDIT)
            for stored in (q_stored, *c_q_stored):
                dve.sem_inc(stored, 16)

            def spread(a, w):
                return a.unsqueeze(2).to_broadcast([P, w, D])

            dve.wait_ge(pool_consts, 9)
            v.tensor_copy(iota_f[:], iota_i[:]).then_inc(chk_step, 1)
            v.tensor_copy(part_f[:], part_i[:]).then_inc(chk_step, 1)
            dve.wait_ge(chk_step, 2)
            v.tensor_copy(iota_ps, iota_f[:, 0:WIN]).then_inc(dve_consts, 1)
            v.tensor_scalar(ident[:], iota_f[:], part_f[:, 0:1], None, ALU.is_equal).then_inc(dve_consts, 1)
            v.tensor_scalar(ident_b[:], iota_f[:], part_f[:, 0:1], None, ALU.is_equal).then_inc(dve_consts, 1)
            v.tensor_scalar(below[:], iota_f[:], part_f[:, 0:1], None, ALU.is_lt).then_inc(dve_consts, 1)
            v.tensor_scalar(dump_f[:], part_f[:], float(DUMP), None, ALU.add).then_inc(chk_step, 1)

            def rsqrt_step(k, y, ssq, half, bits):
                if k == 0:
                    return v.tensor_scalar(ssq, ssq, 1.0 / D, EPS, ALU.mult, ALU.add)
                if k == 1:
                    return v.tensor_scalar(bits, ssq.bitcast(I32), 1, None, ALU.logical_shift_right)
                if k == 2:
                    return v.tensor_scalar(y.bitcast(I32), bits, -1.0, RSQRT_MAGIC, ALU.mult, ALU.add)
                if k == 3:
                    return v.tensor_scalar(half, ssq, -0.5, None, ALU.mult)
                if (k - 4) % 3 == 0:
                    return v.tensor_tensor(ssq, y, y, ALU.mult)
                if (k - 4) % 3 == 1:
                    return v.tensor_tensor(ssq, ssq, half, ALU.mult)
                return v.scalar_tensor_tensor(y, ssq, 1.5, y, ALU.add, ALU.mult)

            def norm_chunk(c, fill):
                xc = x_all[:, bass.ds(c * CH, CH), :]

                def step(k, ins):
                    ins.then_inc(c_step, 1)
                    fill(k)
                    dve.wait_ge(c_step, c * CHUNK_STEPS + (k + CREDIT + 1))

                step(0, v.tensor_reduce(c_tot[:], xc, X, ALU.add))
                v.scalar_tensor_tensor(c_cen[:], spread(c_tot[:], CH), -1.0 / D, xc, ALU.mult, ALU.add)\
                    .then_inc(c_centered, 1)
                fill(1)
                dve.sem_inc(c_step, 1)
                dve.wait_ge(c_squared, done(c))
                step(2, v.tensor_reduce(c_ssq[:], c_sq[:], X, ALU.add))
                for k in range(RSQRT_STEPS):
                    step(3 + k, rsqrt_step(k, c_rstd[:], c_ssq[:], c_half[:], c_bits[:]))
                dve.wait_ge(c_turned, done(2 * c - 1))
                dve.wait_ge(c_h_kept, done(c - 1))
                v.scalar_tensor_tensor(c_h[:], c_cen[:], 0.0, spread(c_rstd[:], CH), ALU.max, ALU.mult)\
                    .then_inc(c_h_ready, 1)

            def split_step_of(k, q, rest, split, step, count, last):
                if k > 0:
                    dve.wait_ge(step, count * SPLIT_STEPS + (k + CREDIT))
                if k == 0:
                    v.tensor_copy(split[:, :, 0:D], q).then_inc(step, 1)
                elif k == 1:
                    v.tensor_tensor(rest, q, split[:, :, 0:D], ALU.subtract).then_inc(step, 1)
                elif k == 2:
                    v.tensor_copy(split[:, :, D:2 * D], rest).then_inc(step, 1)
                else:
                    v.tensor_tensor(split[:, :, 2 * D:3 * D], rest, split[:, :, D:2 * D], ALU.subtract)\
                        .then_inc(last, 1)

            def split_half(c, half, steps=range(SPLIT_STEPS + 1)):
                w0, w = HALVES[half]
                for k in steps:
                    if k == 0:
                        dve.wait_ge(c_kvq_ready, done(c * (CH // 2) + (w0 + w) // 2 - 1))
                        dve.wait_ge(c_q_stored[half], 16 * (c + 1))
                    split_step_of(k, c_kvq[:, w0:w0 + w, 2 * D:3 * D], c_rest[:, w0:w0 + w], c_split[:, w0:w0 + w],
                                  c_split_step, 2 * c + half, c_split_ready)

            def norm_and_split(c, second_half):
                def fill(k):
                    if second_half and k in SECOND_AT:
                        split_half(c - 2, 1, [SECOND_AT.index(k)])
                    if k in FIRST_AT:
                        split_half(c - 1, 0, [FIRST_AT.index(k)])
                norm_chunk(c, fill)

            SECOND_AT = (0, 1, 2, 3)
            FIRST_AT = (8, 10, 12, 14)
            dve.wait_ge(x_loaded[0], 16)
            norm_chunk(0, lambda k: None)
            dve.wait_ge(x_loaded[1], 16)
            norm_and_split(1, second_half=False)
            with dve.Fori(2, CHUNKS) as c:
                norm_and_split(c, second_half=True)
            split_half(CHUNKS - 2, 1)

            cs = [3]

            def chk_link(ins):
                cs[0] += 1
                ins.then_inc(chk_step, 1)
                dve.wait_ge(chk_step, cs[0])

            dve.wait_ge(indices_loaded, 48)
            chk_link(v.tensor_copy(base_f[:], base_all[:]))
            chk_link(v.tensor_copy(limit_f[:], limit_i[:]))
            dve.wait_ge(dst_f_ready, 1)
            chk_link(v.tensor_tensor(rel[:, 0:GROUPS, :], dst_f[:].rearrange("p (g t) -> p g t", t=TILES),
                                     base_f[:].unsqueeze(2).to_broadcast([P, GROUPS, TILES]), ALU.subtract))
            chk_link(v.tensor_tensor(step_f[:, 1:GROUPS], base_f[:, 1:GROUPS], base_f[:, 0:GROUPS - 1], ALU.subtract))
            chk_link(v.memset(carry_rel[:, 0:1], -1.0))
            chk_link(v.tensor_scalar(carry_rel[:, 1:GROUPS], step_f[:, 1:GROUPS], part_f[:, 0:1], -1.0,
                                     ALU.subtract, ALU.mult))
            chk_link(v.tensor_copy(carry_rel[:, GROUPS:GROUPS + 1], carry_rel[:, 0:1]))
            chk_link(v.tensor_copy(rel[:, GROUPS:GROUPS + 2, :], rel[:, 0:2, :]))
            chk_link(v.tensor_reduce(chk[:, 0:1], rel[:, 0:GROUPS, :], mybir.AxisListType.XY, ALU.min))
            chk_link(v.tensor_reduce(chk[:, 3:4], rel[:, 0:GROUPS, :], mybir.AxisListType.XY, ALU.max))
            chk_link(v.tensor_reduce(chk[:, 1:2], step_f[:, 1:GROUPS], X, ALU.min))
            chk_link(v.tensor_tensor(limit_f[:], base_f[:, 6:6 + 4 * (ITERS - LAG - 1) + 1:4], limit_f[:], ALU.subtract))
            chk_link(v.tensor_reduce(chk[:, 2:3], limit_f[:], X, ALU.min))
            chk_link(v.tensor_scalar(chk[:, 3:4], chk[:, 3:4], -1.0, float(WIN - 1), ALU.mult, ALU.add))
            chk_link(v.tensor_reduce(chk[:, 6:7], chk[:, 0:4], X, ALU.min))
            v.tensor_scalar(chk[:, 7:8], chk[:, 6:7], 0.0, None, ALU.is_lt).then_inc(bad_ready, 1)
            dve.wait_ge(bad_summed, 1)
            v.tensor_copy(flag[:], nt_bank[0:1, 0:1]).then_inc(flag_ready, 1)
            split_half(CHUNKS - 1, 0)
            split_half(CHUNKS - 1, 1)
            dve.wait_ge(weights_loaded, 16 * 12)

            def norm_step(k, step, m, w, g, b, last):
                dve.wait_ge(step, m * NORM_STEPS + (k + CREDIT))
                y, c = res[:, 0:w], cen[:, 0:w]
                if k == 1:
                    ins = v.tensor_reduce(tot[:, 0:w], y, X, ALU.add)
                elif k == 2:
                    ins = v.scalar_tensor_tensor(c, spread(tot[:, 0:w], w), -1.0 / D, y, ALU.mult, ALU.add)
                elif k == 3:
                    ins = v.tensor_tensor(sq[:, 0:w], c, c, ALU.mult)
                elif k == 4:
                    ins = v.tensor_reduce(ssq[:, 0:w], sq[:, 0:w], X, ALU.add)
                elif k < 5 + RSQRT_STEPS:
                    ins = rsqrt_step(k - 5, rstd[:, 0:w], ssq[:, 0:w], half[:, 0:w], bits[:, 0:w])
                elif k == 5 + RSQRT_STEPS:
                    ins = v.tensor_tensor(c, c, spread(rstd[:, 0:w], w), ALU.mult)
                elif k == 6 + RSQRT_STEPS:
                    ins = v.tensor_tensor(c, c, g.unsqueeze(1).to_broadcast([P, w, D]), ALU.mult)
                else:
                    ins = v.tensor_tensor(last, c, b.unsqueeze(1).to_broadcast([P, w, D]), ALU.add)
                return ins.then_inc(step, 1)

            def divide_sums(m, w):
                dve.wait_ge(nsum_loaded, 16 * (m + 1))
                v.tensor_scalar(zrec[:, 0:w], nsum[:, 0:w, D:SW], 1e-6, None, ALU.add).then_inc(divide_step, 1)
                dve.wait_ge(divide_step, done(DIVIDE_STEPS * m))
                v.reciprocal(zrec[:, 0:w], zrec[:, 0:w]).then_inc(divide_step, 1)
                dve.wait_ge(divide_step, done(DIVIDE_STEPS * m + 1))
                v.tensor_tensor(attn[:, 0:w].rearrange("p w (h d) -> p w h d", h=H),
                                nsum[:, 0:w, 0:D].rearrange("p w (h d) -> p w h d", h=H),
                                zrec[:, 0:w].unsqueeze(3).to_broadcast([P, w, H, DH]), ALU.mult).then_inc(attn_ready, 1)

            def first_norm(l, j, m, w, steps):
                for k in steps:
                    if k == 0:
                        dve.wait_ge(attn_projected, done(m))
                        v.tensor_tensor(res[:, 0:w], no_bank[:, 0:w * D].rearrange("p (w d) -> p w d", w=w),
                                        h_all[:, bass.ds(j * PAIR, w), :], ALU.add).then_inc(attn_used, 1)
                        dve.wait_ge(attn_used, done(m))
                        dve.sem_inc(norm1_step, 1)
                    elif k < NORM_STEPS - 1:
                        norm_step(k, norm1_step, m, w, norm_sb[:, l, 0, :], norm_sb[:, l, 1, :], h1[:, 0:w])
                    else:
                        dve.wait_ge(norm1_step, m * NORM_STEPS + (k + CREDIT))
                        dve.sem_inc(h1_ready, 1)
                        v.tensor_tensor(h1_b[:, 0:w], h1[:, 0:w], b2_sb[:, l, :].unsqueeze(1).to_broadcast([P, w, D]),
                                        ALU.add).then_inc(norm1_step, 1)

            def second_norm(l, j, m, w, steps):
                xw = x_all[:, bass.ds(j * PAIR, w), :]
                for k in steps:
                    if k == 0:
                        dve.wait_ge(ffn_ready, done(m))
                        dve.wait_ge(norm1_step, (m + 1) * NORM_STEPS + CREDIT)
                        v.tensor_tensor(res[:, 0:w], ffn_of(w).rearrange("p (w d) -> p w d", w=w), h1_b[:, 0:w], ALU.add)\
                            .then_inc(norm2_step, 1)
                    elif k < NORM_STEPS - 1:
                        norm_step(k, norm2_step, m, w, norm_sb[:, l, 2, :], norm_sb[:, l, 3, :],
                                  h2[:, 0:w] if l + 1 < L else sq[:, 0:w])
                    else:
                        dve.wait_ge(norm2_step, m * NORM_STEPS + (k + CREDIT))
                        if l + 1 < L:
                            dve.sem_inc(h2_ready, 1)
                            v.tensor_scalar(h_all[:, bass.ds(j * PAIR, w), :], h2[:, 0:w], 1.0, None, ALU.mult)\
                                .then_inc(norm2_step, 1)
                        else:
                            v.tensor_tensor(xw, sq[:, 0:w], xw, ALU.add).then_inc(norm2_step, 1)
                            dve.wait_ge(norm2_step, m * NORM_STEPS + (k + CREDIT + 1))
                            dve.sem_inc(h2_ready, 1)

            def split_q(m, w, steps=range(SPLIT_STEPS + 1)):
                for k in steps:
                    if k == 0:
                        dve.wait_ge(kvq_staged, done(m))
                        dve.wait_ge(q_stored, 16 * (m + 1))
                    split_step_of(k, kvq[:, 0:w, 2 * D:3 * D], q_rest[:, 0:w], q_split[:, 0:w], split_step, m,
                                  q_split_ready)

            def stage_src(g, s):
                v.tensor_copy(src_slot[:, s % RING, :], src_all[:, bass.ds(g * TILES, TILES)]).then_inc(src_staged, 1)

            def build_onehot(g, s, n):
                dve.wait_ge(group_summed, done(n - RING))
                v.tensor_tensor(onehot[:, s % RING], iota_ps.unsqueeze(1).to_broadcast([P, TILES, WIN]),
                                rel[:, bass.ds(g, 1), :].rearrange("p a t -> p (a t)").unsqueeze(2)
                                .to_broadcast([P, TILES, WIN]), ALU.is_equal).then_inc(onehot_built, 1)

            def build_carry_onehot(g, s):
                v.tensor_scalar(carry_onehot[:, s % RING, :], iota_ps[0:WIN], carry_rel[0:WIN, bass.ds(g, 1)], None,
                                ALU.is_equal).then_inc(carry_onehot_built, 1)

            def use_keys(l, i, s, n, last_pass):
                lacking = (TILES - LAST_TILES) * (l + int(last_pass)) if s == RING - 1 else 0
                dve.wait_ge(kv_gathered[s], 16 * (TILES * (l * ITERS + i + 1) - lacking))
                dve.wait_ge(edge_projected, done(n))
                v.tensor_tensor(prod[:], kv[:, s, :, 0:D], e_bank[:], ALU.mult).then_inc(key_used, 1)

            def use_queries(n):
                dve.wait_ge(query_spread, done(n))
                dve.wait_ge(key_used, done(n))
                v.tensor_tensor(prod[:], prod[:], q_bank[:], ALU.mult).then_inc(query_used, 1)

            def logits(n):
                dve.wait_ge(query_used, done(n))
                v.tensor_reduce(logit[:], prod[:].rearrange("p t (h d) -> p (t h) d", h=H), X, ALU.add)\
                    .then_inc(logit_ready, 1)

            def clip_logits(n):
                dve.wait_ge(logit_ready, done(n))
                v.tensor_scalar(clip[:], logit[:], -5.0 * DH ** 0.5, 5.0 * DH ** 0.5, ALU.max, ALU.min)\
                    .then_inc(clip_ready, 1)

            def messages(s, n):
                dve.wait_ge(score_ready, done(n))
                v.tensor_tensor(msg[:, :, 0:D].rearrange("p t (h d) -> p t h d", h=H),
                                kv[:, s, :, D:2 * D].rearrange("p t (h d) -> p t h d", h=H),
                                msg[:, :, D:SW].unsqueeze(3).to_broadcast([P, TILES, H, DH]),
                                ALU.mult).then_inc(msg_ready, 1)

            def msg_rest_of(s, n):
                dve.wait_ge(msg_hi_ready, done(n))
                v.tensor_tensor(msg_rest[:], msg[:], msg3[:, s % 2, 0], ALU.subtract).then_inc(msg_rest_ready, 1)

            def msg_lo(s, n):
                dve.wait_ge(msg_mid_ready, done(n))
                v.tensor_tensor(msg3[:, s % 2, 2], msg_rest[:], msg3[:, s % 2, 1], ALU.subtract)\
                    .then_inc(msg_lo_ready, 1)

            SPLIT_BY = {0: (0, 0, 0, 1, 2, 3, 4, 4)}
            SECOND_NORM_BY = {1: (0, 0, 0, 1, 2, 4, 6, 10), 2: (11, 13, 14, 16, 18, 20, 22, 22)}
            FIRST_NORM_BY = {2: (0, 0, 0, 0, 0, 0, 0, 4), 3: (5, 7, 9, 11, 13, 15, 17, 22)}
            assert SECOND_NORM_BY[2][-1] == NORM_STEPS and FIRST_NORM_BY[3][-1] == NORM_STEPS

            def steps_at(by, s, gap):
                before = [0] + [k for group in range(s + 1) for k in by.get(group, ())]
                return range(before[gap - 9], before[gap - 8]) if s in by else ()

            dve.wait_ge(flag_ready, 1)
            bad = dve.value_load(flag[0:1, 0:1], min_val=0, max_val=P)
            with dve.If(bad < 1):
                for s in range(IDX_AHEAD):
                    v.tensor_copy(src_slot[:, s, :], src_all[:, s * TILES:(s + 1) * TILES]).then_inc(src_staged, 1)
                build_onehot(0, 0, 0)
                build_onehot(1, 1, 1)
                build_carry_onehot(0, 0)
                for l in range(L):
                    def one_pass(i, edges=True, first=True, second=True, third=True, start=False, last_pass=False,
                                 w=PAIR):
                        m = l * ITEMS + i - LAG
                        b, q = m - 1, m - 2
                        wb = PAIR if first else w
                        wq = PAIR if second else w
                        third = third and l + 1 < L
                        if not edges:
                            if third:
                                split_q(q, wq)
                            if second:
                                second_norm(l, i - LAG - 1, b, wb, range(NORM_STEPS))
                            if first:
                                divide_sums(m, w)
                                first_norm(l, i - LAG, m, w, range(NORM_STEPS))
                            return
                        for s in range(RING):
                            n = l * GROUPS + 4 * i + s
                            behind = not (start and s == 0)

                            def items(gap):
                                if third:
                                    split_q(q, wq, steps_at(SPLIT_BY, s, gap))
                                if second:
                                    second_norm(l, i - LAG - 1, b, wb, steps_at(SECOND_NORM_BY, s, gap))
                                if first:
                                    first_norm(l, i - LAG, m, w, steps_at(FIRST_NORM_BY, s, gap))

                            use_keys(l, i, s, n, last_pass)
                            stage_src(4 * i + s + IDX_AHEAD, s + IDX_AHEAD)
                            items(0)
                            if behind:
                                msg_rest_of(s - 1, n - 1)
                            items(1)
                            use_queries(n)
                            items(2)
                            logits(n)
                            items(3)
                            if behind:
                                msg_lo(s - 1, n - 1)
                            clip_logits(n)
                            items(4)
                            build_onehot(4 * i + s + 2, s + 2, n + 2)
                            items(5)
                            messages(s, n)
                            items(6)
                            build_carry_onehot(4 * i + s + 1, s + 1)
                            items(7)
                            if first and s == 0:
                                divide_sums(m, w)

                    one_pass(0, first=False, second=False, third=False, start=True)
                    one_pass(1, first=False, second=False, third=False)
                    one_pass(2, second=False, third=False)
                    one_pass(3, third=False)
                    with dve.Fori(LAG + 2, ITERS - 1) as i:
                        one_pass(i)
                    one_pass(ITERS - 1, last_pass=True)
                    msg_rest_of(RING - 1, (l + 1) * GROUPS - 1)
                    msg_lo(RING - 1, (l + 1) * GROUPS - 1)
                    one_pass(ITERS, edges=False, w=QUAD)
                    one_pass(ITERS + 1, edges=False, first=False, w=QUAD)
                    one_pass(ITERS + 2, edges=False, first=False, second=False, w=QUAD)
            with dve.Else():
                for l in range(L):
                    with dve.Fori(0, EDGE_TILES) as t:
                        n = l * EDGE_TILES + t

                        def step(k, ins):
                            ins.then_inc(g_step, 1)
                            dve.wait_ge(g_step, n * G_STEPS + (k + 1))

                        step(0, v.tensor_copy(g_src[:], src_all[:, bass.ds(t, 1)]))
                        step(1, v.tensor_copy(g_dst[:], dst_all[:, bass.ds(t, 1)]))
                        step(2, v.tensor_copy(g_dstf[:], dst_f[:, bass.ds(t, 1)]))
                        v.tensor_copy(g_bc[:], g_dstf[:].to_broadcast([P, P])).then_inc(g_indexed, 1)
                        dve.wait_ge(g_projected, n + 1)
                        step(3, v.tensor_scalar(g_same[:], acc_bank[:, 0:P], g_dstf[:, 0:1], None, ALU.is_equal))
                        step(4, v.tensor_tensor(g_tmp[:], g_same[:], below[:], ALU.mult))
                        step(5, v.tensor_reduce(g_dup[:, 0:1], g_tmp[:], X, ALU.max))
                        step(6, v.tensor_tensor(g_dup[:, 1:2], dump_f[:], g_dstf[:], ALU.subtract))
                        step(7, v.tensor_tensor(g_dup[:, 1:2], g_dup[:, 1:2], g_dup[:, 0:1], ALU.mult))
                        step(8, v.tensor_tensor(g_to[:], g_dup[:, 1:2], g_dstf[:], ALU.add))
                        dve.wait_ge(g_gathered[l], 32 * (t + 1))
                        step(9, v.tensor_tensor(g_q[:], g_q3[:, 0:D], g_q3[:, D:2 * D], ALU.add))
                        step(10, v.tensor_tensor(g_q[:], g_q[:], g_q3[:, 2 * D:3 * D], ALU.add))
                        v.tensor_tensor(prod[:, 0, :], g_kv[:, 0:D], e_bank[:, 0, :], ALU.mult).then_inc(key_used, 1)
                        dve.wait_ge(key_used, done(n))
                        v.tensor_tensor(prod[:, 0, :], prod[:, 0, :], g_q[:], ALU.mult).then_inc(query_used, 1)
                        dve.wait_ge(query_used, done(n))
                        v.tensor_reduce(logit[:, 0:H], prod[:, 0, :].rearrange("p (h d) -> p h d", h=H), X, ALU.add)\
                            .then_inc(logit_ready, 1)
                        dve.wait_ge(logit_ready, done(n))
                        v.tensor_scalar(clip[:, 0:H], logit[:, 0:H], -5.0 * DH ** 0.5, 5.0 * DH ** 0.5, ALU.max, ALU.min)\
                            .then_inc(g_clipped, 1)
                        dve.wait_ge(g_scored, n + 1)
                        v.tensor_tensor(g_msg[:, 0:D].rearrange("p (h d) -> p h d", h=H),
                                        g_kv[:, D:2 * D].rearrange("p (h d) -> p h d", h=H),
                                        g_msg[:, D:SW].unsqueeze(2).to_broadcast([P, H, DH]), ALU.mult)\
                            .then_inc(g_msg_ready, 1)
                        dve.wait_ge(g_summed, n + 1)
                        v.tensor_copy(g_sum[:], q_bank[:].rearrange("p t d -> p (t d)")[:, 0:SW]).then_inc(g_sum_ready, 1)
                        dve.wait_ge(g_added[l], 16 * (t + 1))

                    def one_item(j, m, w):
                        divide_sums(m, w)
                        first_norm(l, j, m, w, range(NORM_STEPS))
                        second_norm(l, j, m, w, range(NORM_STEPS))
                        if l + 1 < L:
                            split_q(m, w)

                    with dve.Fori(0, LAST) as j:
                        one_item(j, l * ITEMS + j, PAIR)
                    one_item(LAST, l * ITEMS + LAST, QUAD)


_WEIGHTS = ("WE", "WO", "bO", "ln1_g", "ln1_b", "W1", "b1", "W2", "b2", "ln2_g", "ln2_b")


def kernel(**inputs):
    import concourse.bacc as _bacc
    from concourse.bass_utils import run_bass_kernel_spmd as _run

    def get(name):
        return np.asarray(inputs[name])

    x = np.zeros((NP_, D), np.float32)
    x[:N] = get("x")
    x = x.reshape(WINDOWS, P, D).transpose(1, 0, 2)
    src = np.zeros(EP, np.int32)
    src[:E] = get("src")
    src = src.reshape(EDGE_TILES, P).T
    src = np.concatenate([src, src[:, :IDX_AHEAD * TILES]], axis=1)
    dst = np.full(EP, NP_ - 1, np.int32)
    dst[:E] = get("dst")
    base = dst[::GE]
    dst = dst.reshape(EDGE_TILES, P).T
    attr = np.zeros((EP, D), np.float32)
    attr[:E] = get("edge_attr_64")
    attr = attr.reshape(GROUPS, 2, GE // 2, D).transpose(0, 1, 3, 2)
    wkvq = np.concatenate([get("L0_gnn_WK"), get("L0_gnn_WV"), get("L0_gnn_WQ")], axis=2)
    w = {k: get("L0_gnn_" + k) for k in _WEIGHTS}
    w["b1"] = w["b1"].T
    arrays = dict(x=x, src=src, dst=dst, base=base, edge_attr_t=attr, wkvq=wkvq, we=w["WE"], wo=w["WO"], bo=w["bO"],
                  g1=w["ln1_g"], be1=w["ln1_b"], w1=w["W1"], b1=w["b1"], w2=w["W2"], b2=w["b2"], g2=w["ln2_g"],
                  be2=w["ln2_b"])

    nc = _bacc.Bacc("TRN2", target_bir_lowering=False, num_devices=1)
    maps, aps = {}, {}
    for name, a in arrays.items():
        a = np.ascontiguousarray(a)
        maps[f"in_{name}"] = a
        aps[name] = nc.dram_tensor(f"in_{name}", a.shape, mybir.dt.from_np(a.dtype), kind="ExternalInput").ap()
    aps["out"] = nc.dram_tensor("out_nodes", (P, WINDOWS, D), F32, kind="ExternalOutput").ap()
    gnn(nc, **aps)
    r = _run(nc, [maps], core_ids=[0])
    got = np.asarray(r.results[0]["out_nodes"])
    return got.transpose(1, 0, 2).reshape(NP_, D)[:N]
```
